# Optimizing a Trainium2 kernel written in Bass

```python
import numpy as np
import jax
import jax.numpy as jnp

def _softmax(x, axis=-1):
    return jax.nn.softmax(x, axis=axis)

def _gelu(x):
    return jax.nn.gelu(x, approximate=True)

def _silu(x):
    return jax.nn.silu(x)

def _sigmoid(x):
    return jax.nn.sigmoid(x)

def _layernorm(x, axis=-1, eps=1e-05):
    m = jnp.mean(x, axis=axis, keepdims=True)
    v = jnp.var(x, axis=axis, keepdims=True)
    return (x - m) / jnp.sqrt(v + eps)

def _scatter_add(tgt, idx, src, axis=0):
    return tgt.at[idx].add(src)

def _segment_sum(src, seg, n):
    return jax.ops.segment_sum(src, seg, n)
kernel_name = 'mk_metaformer_d1_conv_nchw128_r2_fd9990'

def setup_inputs(seed: int=0):
    np.random.seed(seed)
    _w = jnp.asarray

    def _rec_inputs():
        import jax
        import jax.numpy as jnp
        _gk = jax.random.key(seed)
        x = -0.0001142 + 0.9999 * jax.random.normal(jax.random.fold_in(_gk, 1), (16, 64, 36, 100), jnp.float32)
        return x
    x = _rec_inputs()

    def _L0_conv_setup():
        import jax, jax.numpy as jnp
        import numpy as np
        B, C, H, W = (16, 64, 36, 100)
        K, PAD = (9, 4)

        def conv1d(x, w):
            return jax.lax.conv_general_dilated(x, w, window_strides=(1,), padding=[(PAD, PAD)], dimension_numbers=('NCH', 'OIH', 'NCH'))

        def sweep_fwd(seq, w):

            def step(carry, row):
                new = row + jax.nn.relu(conv1d(carry, w))
                return (new, new)
            _, out = jax.lax.scan(step, seq[0], seq[1:])
            return jnp.concatenate([seq[:1], out], axis=0)

        def sweep_bwd(seq, w):
            rev = seq[::-1]

            def step(carry, row):
                new = row + jax.nn.relu(conv1d(carry, w))
                return (new, new)
            _, out = jax.lax.scan(step, rev[0], rev[1:-1])
            return jnp.concatenate([seq[:1], out[::-1], seq[-1:]], axis=0)
        key = jax.random.key(seed)
        kx, kd, ku, kr, kl = jax.random.split(key, 5)
        s = 0.03
        return {'x': jax.random.normal(kx, (B, C, H, W), jnp.float32), 'w_d': jax.random.normal(kd, (C, C, 1, K), jnp.float32) * s, 'w_u': jax.random.normal(ku, (C, C, 1, K), jnp.float32) * s, 'w_r': jax.random.normal(kr, (C, C, K, 1), jnp.float32) * s, 'w_l': jax.random.normal(kl, (C, C, K, 1), jnp.float32) * s}
    _L0_conv_all = _L0_conv_setup()
    _L0_conv_in = {k: v for k, v in _L0_conv_all.items() if k in ('w_d', 'w_u', 'w_r', 'w_l')}
    del _L0_conv_all

    def _L0_ffn_setup():
        import jax, jax.numpy as jnp
        import numpy as np
        B, N, D, C, E, K = (8, 4096, 64, 64, 8, 2)
        key = jax.random.key(seed)
        k0, k1, k2 = jax.random.split(key, 3)
        x = jax.random.normal(k0, (B, N, D), dtype=jnp.float32)
        router_w = jax.random.normal(k1, (D, E), dtype=jnp.float32) * 0.05
        router_b = jnp.zeros((E,), dtype=jnp.float32)
        expert_w = jax.random.normal(k2, (E, D, C), dtype=jnp.float32) * (1.0 / np.sqrt(D))
        expert_b = jnp.zeros((E, C), dtype=jnp.float32)
        return {'x': x, 'router_w': router_w, 'router_b': router_b, 'expert_w': expert_w, 'expert_b': expert_b}
    _L0_ffn_all = _L0_ffn_setup()
    _L0_ffn_in = {k: v for k, v in _L0_ffn_all.items() if k in ('router_w', 'router_b', 'expert_w', 'expert_b')}
    del _L0_ffn_all
    return {'x': x, 'L0_conv_w_d': _L0_conv_in['w_d'], 'L0_conv_w_u': _L0_conv_in['w_u'], 'L0_conv_w_r': _L0_conv_in['w_r'], 'L0_conv_w_l': _L0_conv_in['w_l'], 'L0_ffn_router_w': _L0_ffn_in['router_w'], 'L0_ffn_router_b': _L0_ffn_in['router_b'], 'L0_ffn_expert_w': _L0_ffn_in['expert_w'], 'L0_ffn_expert_b': _L0_ffn_in['expert_b']}

def reference(x, L0_conv_w_d, L0_conv_w_u, L0_conv_w_r, L0_conv_w_l, L0_ffn_router_w, L0_ffn_router_b, L0_ffn_expert_w, L0_ffn_expert_b):
    import jax
    import jax.numpy as jnp

    def _L0_conv_ref(x, w_d, w_u, w_r, w_l):
        import jax, jax.numpy as jnp
        import numpy as np
        B, C, H, W = (16, 64, 36, 100)
        K, PAD = (9, 4)

        def conv1d(x, w):
            return jax.lax.conv_general_dilated(x, w, window_strides=(1,), padding=[(PAD, PAD)], dimension_numbers=('NCH', 'OIH', 'NCH'))

        def sweep_fwd(seq, w):

            def step(carry, row):
                new = row + jax.nn.relu(conv1d(carry, w))
                return (new, new)
            _, out = jax.lax.scan(step, seq[0], seq[1:])
            return jnp.concatenate([seq[:1], out], axis=0)

        def sweep_bwd(seq, w):
            rev = seq[::-1]

            def step(carry, row):
                new = row + jax.nn.relu(conv1d(carry, w))
                return (new, new)
            _, out = jax.lax.scan(step, rev[0], rev[1:-1])
            return jnp.concatenate([seq[:1], out[::-1], seq[-1:]], axis=0)
        wd = w_d[:, :, 0, :]
        wu = w_u[:, :, 0, :]
        wr = w_r[:, :, :, 0]
        wl = w_l[:, :, :, 0]
        rows = jnp.transpose(x, (2, 0, 1, 3))
        rows = sweep_fwd(rows, wd)
        rows = sweep_bwd(rows, wu)
        x = jnp.transpose(rows, (1, 2, 0, 3))
        cols = jnp.transpose(x, (3, 0, 1, 2))
        cols = sweep_fwd(cols, wr)
        cols = sweep_bwd(cols, wl)
        return jnp.transpose(cols, (1, 2, 3, 0))

    def _L0_ffn_ref(x, router_w, router_b, expert_w, expert_b):
        import jax, jax.numpy as jnp
        import numpy as np
        B, N, D, C, E, K = (8, 4096, 64, 64, 8, 2)
        router_probs = jax.nn.softmax(x @ router_w + router_b, axis=-1)
        top_p, top_i = jax.lax.top_k(router_probs, K)
        top_p = top_p / jnp.sum(top_p, axis=-1, keepdims=True)
        expert_out = jnp.einsum('bnd,edc->bnec', x, expert_w) + expert_b
        gathered = jnp.take_along_axis(expert_out, top_i[..., None], axis=2)
        return jnp.einsum('bnk,bnkc->bnc', top_p, gathered)

    def _gn(v, G=32, eps=1e-05):
        B_, C_, H_, W_ = v.shape
        g = v.reshape(B_, G, C_ // G, H_, W_)
        m = jnp.mean(g, axis=(2, 3, 4), keepdims=True)
        s = jnp.var(g, axis=(2, 3, 4), keepdims=True)
        return ((g - m) / jnp.sqrt(s + eps)).reshape(v.shape)

    def _ln_c(v, eps=1e-06):
        m = jnp.mean(v, axis=1, keepdims=True)
        s = jnp.var(v, axis=1, keepdims=True)
        return (v - m) / jnp.sqrt(s + eps)

    def _ln_t(v, eps=1e-05):
        m = jnp.mean(v, axis=-1, keepdims=True)
        s = jnp.var(v, axis=-1, keepdims=True)
        return (v - m) / jnp.sqrt(s + eps)

    def _to_tokens(v):
        B_, C_, H_, W_ = v.shape
        return v.reshape(B_, C_, H_ * W_).transpose(0, 2, 1)

    def _from_tokens(t, like):
        B_, C_, H_, W_ = like.shape
        return t.transpose(0, 2, 1).reshape(B_, C_, H_, W_)
    x = x + _L0_conv_ref(_ln_c(x), L0_conv_w_d, L0_conv_w_u, L0_conv_w_r, L0_conv_w_l)
    t = _to_tokens(x)
    t = t + _L0_ffn_ref(_ln_t(t), L0_ffn_router_w, L0_ffn_router_b, L0_ffn_expert_w, L0_ffn_expert_b)
    x = _from_tokens(t, x)
    return x

_drawn_inputs = setup_inputs


def setup_inputs(seed=0):
    import zlib

    import numpy as np

    out = dict(_drawn_inputs(seed))
    spreads = {'L0_ffn_router_b': (0.0, 0.1), 'L0_ffn_expert_b': (0.0, 0.368)}
    factors = {}
    for name, (base, spread) in spreads.items():
        noise = np.random.default_rng([zlib.crc32(name.encode()), seed]).standard_normal(out[name].shape)
        drawn = base * np.exp(spread * noise) if base else spread * noise
        out[name] = jnp.asarray(drawn.astype(out[name].dtype))
    for name, factor in factors.items():
        out[name] = (out[name] * factor).astype(out[name].dtype)
    return out
```

```python
from contextlib import ExitStack

import concourse.bass as bass
from concourse import mybir

F32 = mybir.dt.float32
F32R = mybir.dt.float32r
ALU = mybir.AluOpType
ACT = mybir.ActivationFunctionType
AX = mybir.AxisListType


def metaformer_kernel(nc, x, w_d, w_u, w_r, w_l, router_w, router_b, expert_w, expert_b, out):
    B, C, H, W = x.shape
    TAPS = w_d.shape[-1]
    E = expert_w.shape[0]
    P = 2 * C
    HP, WP = H // 2, W // 2
    SH = TAPS // 2 + 1
    SHIFTS = [0, -1, 1, -2, 2]
    TAPE = TAPS + 1
    G = 2
    BG = B // G
    REG = B * W
    NV, NH = BG * WP, HP * BG
    CH = 4
    BC = B // CH
    NC = REG // CH
    TN = 128
    TILES = -(-REG // TN)
    TAIL = REG - (TILES - 1) * TN
    NG = TILES * 2
    BIG = 1.0e30

    ctx = ExitStack()
    with ctx:
        def sb(name, shape, dt=F32):
            return ctx.enter_context(nc.sbuf_tensor(name, shape, dt))

        def sem(name):
            return ctx.enter_context(nc.semaphore(name))

        act_buf = sb("act_buf", [P, HP * REG])
        rows = act_buf[:, :].rearrange("p (h b w) -> p h b w", h=H, b=B)
        cols = act_buf[:, :].rearrange("p (j b w) -> p j b w", j=HP, b=B)
        x_in = sb("x_in", [P, 2, B, W])
        parts = sb("parts", [P, 2 * 2 * REG], F32R)
        nwv = SH * P
        vw = parts[:, 0:4 * nwv].rearrange("p (k l s m) -> p k l s m", k=2, l=2, s=SH)
        NPAD = BG * (WP + 2)
        carry = parts[:, 4 * nwv:4 * nwv + 2 * G * NPAD].rearrange("p (l g b w) -> p l g b w", l=2, g=G, b=BG)
        tok = parts[:, :].rearrange("p (s l n) -> p s l n", s=2, l=2)
        NSM = NG * E
        scratch = sb("scratch", [P, 2 * E * P + 9 * NSM])
        raw_w = scratch[:, 0:4 * C * TAPS].rearrange("p (k n) -> p k n", k=4)
        tape = act_buf[:, (HP * REG - 4 * C * TAPE):].rearrange("p (k t c) -> p k t c", k=4, t=TAPE)
        new_row = scratch[:, 0:2 * 2 * G * NV].rearrange("p (a q g n) -> p a q g n", a=2, q=2, g=G)
        gated = scratch[:, 0:2 * E * P].rearrange("p (a e m) -> p a e m", a=2, e=E)
        sm = scratch[:, 2 * E * P:].rearrange("p (k n e) -> p k n e", k=9, e=E)
        logit, hit, first, rest, second, gate1, gate2 = (sm[:, k] for k in range(7))
        gate = [sm[:, 7], sm[:, 8]]
        hw = sb("hw", [P, 2, SH, P])
        kbuf = sb("kbuf", [P, G, HP, BG])
        sq = sb("sq", [P, 2, NC])
        lnv = sb("lnv", [P, 2, NC])
        rstd = sb("rstd", [P, 2, NC])
        xn = sb("xn", [P, 2, NC])
        ident = sb("ident", [P, P])
        mean_w = sb("mean_w", [P, P])
        center_w = sb("center_w", [P, P])
        eps_c = sb("eps_c", [P, 2])
        rank_w = sb("rank_w", [P, NG, E])
        ew = sb("ew", [P, E * C + E])
        eb = sb("eb", [P, E * C + E])
        em = sb("em", [P, 2, E * C], F32R)
        rm_f = sb("rm_f", [P, P])
        rm = sb("rm", [P, 2, P], F32R)
        logit_c = sb("logit_c", [2 * E, REG])
        best = sb("best", [P, 6, NG])

        banks = [ctx.enter_context(nc.psum_tensor(f"bank{i}", [P, 512], F32)) for i in range(8)]

        s_wraw = sem("s_wraw")
        s_eraw = sem("s_eraw")
        s_x = [sem("s_x0"), sem("s_x1")]
        s_id0 = sem("s_id0")
        s_id = sem("s_id")
        s_cst = sem("s_cst")
        s_tape0 = sem("s_tape0")
        s_tape = sem("s_tape")
        s_wt = sem("s_wt")
        s_wh = sem("s_wh")
        s_wv = sem("s_wv")
        s_cmean = sem("s_cmean")
        s_em = sem("s_em")
        s_d = sem("s_d")
        s_sq = sem("s_sq")
        s_v = sem("s_v")
        s_ln = sem("s_ln")
        s_r = sem("s_r")
        s_xn = sem("s_xn")
        s_h = [sem(f"s_h{g}") for g in range(G)]
        s_l = [sem(f"s_l{g}") for g in range(G)]
        s_mm = [sem(f"s_mm{g}") for g in range(G)]
        s_new = [sem(f"s_new{g}") for g in range(G)]
        s_trv = sem("s_trv")
        s_tra = sem("s_tra")
        s_k = [sem(f"s_k{g}") for g in range(G)]
        s_hm = [sem(f"s_hm{g}") for g in range(G)]
        s_cb = [sem(f"s_cb{g}") for g in range(G)]
        s_t = sem("s_t")
        s_d2 = sem("s_d2")
        s_sq2 = sem("s_sq2")
        s_v2 = sem("s_v2")
        s_ln2 = sem("s_ln2")
        s_r2 = sem("s_r2")
        s_xn2 = sem("s_xn2")
        s_th = sem("s_th")
        s_tl = sem("s_tl")
        s_lg = sem("s_lg")
        s_lc = sem("s_lc")
        s_lt = sem("s_lt")
        s_sm = sem("s_sm")
        s_ex = sem("s_ex")
        s_p = sem("s_p")
        s_g = sem("s_g")
        s_y = sem("s_y")
        s_o = sem("s_o")
        s_out = sem("s_out")

        block = ctx.enter_context(nc.Block())

        def pair_view(dram, j, q):
            return dram.rearrange("b c (j q) w -> q j c b w", q=2)[q, j]

        @block.sync
        def _(sp):
            def load(j, slot):
                for q in range(2):
                    sp.dma_start(x_in[q * C:(q + 1) * C, slot], pair_view(x, j, q)).then_inc(s_x[slot], 16)

            load(0, 0)
            load(1, 1)
            with sp.Fori(1, HP // 2) as i:
                for slot in range(2):
                    sp.wait_ge(s_d, 2 * CH * i - CH + CH * slot)
                    load(2 * i + slot, slot)
            for slot in range(2):
                sp.wait_ge(s_d, CH * (HP - 1 + slot))
                load(slot, slot)

            def store(j):
                sp.wait_ge(s_o, 2 + TILES * (j + 1))
                for q in range(2):
                    sp.dma_start(pair_view(out, j, q), cols[q * C:(q + 1) * C, j]).then_inc(s_out, 16)

            with sp.Fori(0, HP // 2 - 1) as i:
                for slot in range(2):
                    sp.wait_ge(s_t, CH * (2 * i + slot + 1))
                    load(2 * i + slot + 2, slot)
                    store(2 * i + slot)
            store(HP - 2)
            store(HP - 1)
            sp.wait_ge(s_out, HP * 32)

        @block.gpsimd
        def _(pool):
            nc.gpsimd.memset(ident[:, :], 0.0).then_inc(s_id0, 1)
            pool.wait_ge(s_id0, 1)
            nc.gpsimd.affine_select(out=ident[:, :], in_=ident[:, :], compare_op=ALU.not_equal, fill=1.0,
                                    base=0, pattern=[[-1, P]], channel_multiplier=1).then_inc(s_id, 1)

        SMN = 19
        NCST = 4 + E + 2 + 1

        @block.scalar
        def _(act):
            for k, w in enumerate((w_d, w_u, w_r, w_l)):
                flat = w.rearrange("o i a b -> o (i a b)")
                for q in range(2):
                    act.dma_start(raw_w[q * C:(q + 1) * C, k], flat).then_inc(s_wraw, 16)
            for q in range(2):
                half = slice(q * C, (q + 1) * C)
                act.dma_start(ew[half, 0:E * C].rearrange("p (e c) -> p e c", e=E),
                              expert_w.rearrange("e d c -> d e c")).then_inc(s_eraw, 16)
                act.dma_start(ew[half, E * C:], router_w).then_inc(s_eraw, 16)
            act.dma_start(eb[:, 0:E * C],
                          expert_b.rearrange("(o e) c -> o (e c)", o=1).broadcast_to([P, E * C])).then_inc(s_eraw, 16)
            act.dma_start(eb[:, E * C:], router_b.rearrange("(o e) -> o e", o=1).broadcast_to([P, E])).then_inc(s_eraw, 16)
            nc.scalar.preload_act_table_set("natural_log_exp_and_others")
            for n in range(8):
                k = n // 2
                act.wait_ge(s_wt, n + 1)
                lo, hi = (0, 4) if n % 2 == 0 else (4, SH)
                dst = vw[:, k, 0, lo:hi] if k < 2 else hw[:, k - 2, lo:hi]
                act.activation(dst, banks[n][:, 0:(hi - lo) * P].rearrange("p (s m) -> p s m", m=P),
                               ACT.Copy).then_inc(s_wh, 1)

            def square(n, b):
                act.wait_ge(s_d, n + 1)
                act.activation(sq[:, b], banks[b][:, 0:NC], ACT.Square).then_inc(s_sq, 1)

            def inv_std(n, b):
                act.wait_ge(s_v, n + 1)
                act.wait_ge(s_xn, n + 1)
                act.activation(lnv[:, b], banks[2 + b][:, 0:NC], ACT.Ln, bias=eps_c[:, 0:1]).then_inc(s_ln, 1)
                act.wait_ge(s_ln, n + 1)
                act.activation(rstd[:, b], lnv[:, b], ACT.Exp, scale=-0.5).then_inc(s_r, 1)

            act.wait_ge(s_cst, NCST)
            with act.Fori(0, HP // 2) as i:
                for k in range(2 * CH + 1):
                    if k < 2 * CH:
                        square(2 * CH * i + k, k % 2)
                    if k >= 1:
                        inv_std(2 * CH * i + k - 1, (k - 1) % 2)

            act.wait_ge(s_xn, 2 + HP * CH)
            for g in range(G):
                act.activation(carry[:, 0, g, :, 1:WP + 1],
                               rows[:, 0, g * BG:(g + 1) * BG], ACT.Copy).then_inc(s_h[g], 1)
            with act.Fori(1, H) as t:
                for g in range(G):
                    act.wait_ge(s_new[g], t)
                    act.activation(carry[:, 0, g, :, 1:WP + 1],
                                   rows[:, t, g * BG:(g + 1) * BG], ACT.Copy).then_inc(s_h[g], 1)

            def round_row(t, par, q):
                for g in range(G):
                    act.wait_ge(s_new[g], t)
                    act.activation(carry[:, 0, g, :, 1:WP + 1],
                                   new_row[:, par, q, g].rearrange("p (b w) -> p b w", b=BG), ACT.Copy).then_inc(s_h[g], 1)

            def move_cross(j, par):
                for g in range(G):
                    for q in range(2):
                        dst = cols[q * C:(q + 1) * C, j, g * BG:(g + 1) * BG].rearrange("p b (w a) -> p b w a", a=2)[:, :, :, 1 - q]
                        src = new_row[(1 - q) * C:(2 - q) * C, par, q, g].rearrange("p (b w) -> p b w", b=BG)
                        act.activation(dst, src, ACT.Copy).then_inc(s_tra, 1)

            round_row(H, 1, 0)
            act.wait_ge(s_trv, G)
            move_cross(HP - 1, 1)
            with act.Fori(0, (HP - 2) // 2) as i:
                for par in range(2):
                    t = 4 * i + 2 * par + H + 1
                    round_row(t, par, 1)
                    round_row(t + 1, par, 0)
                    move_cross(HP - 2 - par - 2 * i, par)
            round_row(2 * H - 3, 0, 1)
            for g in range(G):
                act.wait_ge(s_new[g], 2 * H - 2)
            move_cross(0, 0)

            def copy_back(u, w):
                for g in range(G):
                    act.wait_ge(s_k[g], u + 1)
                    act.activation(cols[:, :, g * BG:(g + 1) * BG, w], kbuf[:, g], ACT.Copy).then_inc(s_cb[g], 1)

            with act.Fori(1, W) as u:
                copy_back(u, u)
            with act.Fori(W, 2 * W - 2) as u:
                w = u * -1 + (2 * W - 2)
                copy_back(u, w)

            def norm_square(j, c):
                act.wait_ge(s_d2, CH * j + c + 1)
                act.activation(sq[:, 0], banks[0][:, 0:NC], ACT.Square).then_inc(s_sq2, 1)

            def norm_std(j, c):
                n = CH * j + c
                act.wait_ge(s_v2, n + 1)
                act.wait_ge(s_xn2, n)
                act.activation(lnv[:, 0], banks[1][:, 0:NC], ACT.Ln, bias=eps_c[:, 1:2]).then_inc(s_ln2, 1)
                act.wait_ge(s_ln2, n + 1)
                act.activation(rstd[:, 0], lnv[:, 0], ACT.Exp, scale=-0.5).then_inc(s_r2, 1)

            def round_tokens(j, slot, c):
                act.wait_ge(s_xn2, CH * j + c + 1)
                act.activation(tok[:, slot, 0, c * NC:(c + 1) * NC], xn[:, 0], ACT.Identity,
                               bias=1.0).then_inc(s_th, 1)

            def take_logits(j, c):
                act.wait_ge(s_lg, CH * j + c + 1)
                act.activation(logit_c[:, c * NC:(c + 1) * NC], banks[2][0:2 * E, 0:NC], ACT.Copy).then_inc(s_lc, 1)

            def exponential(j):
                act.wait_ge(s_sm, SMN * j + 12)
                act.activation(best[:, 3], best[:, 2], ACT.Exp).then_inc(s_ex, 1)

            def tokens(j, slot, reused):
                for c in range(CH):
                    if c == 0:
                        norm_square(j, 0)
                        norm_std(j, 0)
                        if reused:
                            act.wait_ge(s_p, 2 * TILES * (j - 1))
                    round_tokens(j, slot, c)
                    if c < CH - 1:
                        norm_square(j, c + 1)
                    take_logits(j, c)
                    if c < CH - 1:
                        norm_std(j, c + 1)
                exponential(j)

            tokens(0, 0, False)
            tokens(1, 1, False)
            with act.Fori(1, HP // 2) as i:
                for slot in range(2):
                    tokens(2 * i + slot, slot, True)


        @block.vector
        def _(dve):
            nc.vector.memset(best[:, :, :], 0.0).then_inc(s_xn, 2)
            nc.vector.memset(tape, 0.0).then_inc(s_tape0, 1)
            nc.vector.memset(parts[:, 4 * nwv:4 * nwv + 2 * G * NPAD].bitcast(F32), 0.0).then_inc(s_tape0, 1)
            nc.vector.memset(rm_f[:, :], 0.0).then_inc(s_g, 2)
            nc.vector.memset(lnv[:, 0, 0:1], 0.0).then_inc(s_o, 2)
            nc.vector.memset(lnv[:, 0, 1:2], 0.0).then_inc(s_tra, 1)
            for g in range(G):
                nc.vector.memset(lnv[:, 1, g:g + 1], 0.0).then_inc(s_cb[g], 1)
            for q in range(2):
                for a in range(2):
                    nc.vector.memset(mean_w[q * C:(q + 1) * C, a * C:(a + 1) * C],
                                     1.0 / C if a == q else 0.0).then_inc(s_cst, 1)
            for e in range(E):
                nc.vector.memset(rank_w[:, :, e], float(E - e)).then_inc(s_cst, 1)
            nc.vector.memset(eps_c[:, 0:1], 1.0e-6).then_inc(s_cst, 1)
            nc.vector.memset(eps_c[:, 1:2], 1.0e-5).then_inc(s_cst, 1)
            dve.wait_ge(s_id, 1)
            dve.wait_ge(s_cst, 4)
            nc.vector.tensor_tensor(center_w[:, :], ident[:, :], mean_w[:, :], ALU.subtract).then_inc(s_cst, 1)
            dve.wait_ge(s_wraw, 8 * 16)
            dve.wait_ge(s_tape0, 2)
            for k in range(4):
                for q in range(2):
                    nc.vector.tensor_copy(tape[q * C:(q + 1) * C, k, q:q + TAPS],
                                          raw_w[q * C:(q + 1) * C, k].rearrange("p (c t) -> p t c", t=TAPS)).then_inc(s_tape, 1)
            for n in range(4):
                lo, hi = (0, 4) if n % 2 == 0 else (4, SH)
                dve.wait_ge(s_wh, n + 1)
                nc.vector.tensor_tensor(vw[:, n // 2, 1, lo:hi], banks[n][:, 0:(hi - lo) * P].rearrange("p (s m) -> p s m", m=P),
                                        vw[:, n // 2, 0, lo:hi].bitcast(F32), ALU.subtract).then_inc(s_wv, 1)
            dve.wait_ge(s_cmean, 1)
            dve.wait_ge(s_eraw, 6 * 16)
            nc.vector.tensor_tensor(ew[:, 0:E * C], ew[:, 0:E * C], banks[0][:, 0:E * C], ALU.subtract).then_inc(s_em, 1)
            nc.vector.tensor_tensor(ew[:, E * C:], ew[:, E * C:], banks[1][:, 0:E], ALU.subtract).then_inc(s_em, 1)
            dve.wait_ge(s_em, 2)
            nc.vector.scalar_tensor_tensor(ew[:, :], eb[:, :], 1.0 / C, ew[:, :], ALU.mult, ALU.add).then_inc(s_em, 1)
            dve.wait_ge(s_em, 3)
            dve.wait_ge(s_g, 2)
            nc.vector.tensor_copy(em[:, 0], ew[:, 0:E * C]).then_inc(s_em, 1)
            for q in range(2):
                nc.vector.tensor_copy(rm_f[q * C:(q + 1) * C, q * E:(q + 1) * E], ew[q * C:(q + 1) * C, E * C:]).then_inc(s_em, 1)
            dve.wait_ge(s_em, 6)
            nc.vector.tensor_tensor(em[:, 1], ew[:, 0:E * C], em[:, 0].bitcast(F32), ALU.subtract).then_inc(s_em, 1)
            nc.vector.tensor_copy(rm[:, 0], rm_f[:, :]).then_inc(s_em, 1)
            dve.wait_ge(s_em, 8)
            nc.vector.tensor_tensor(rm[:, 1], rm_f[:, :], rm[:, 0].bitcast(F32), ALU.subtract).then_inc(s_em, 1)

            with dve.Fori(0, HP // 2) as i:
                for k in range(2 * CH):
                    n = 2 * CH * i + k
                    b, j, c = k % 2, 2 * i + k // CH, k % CH
                    dve.wait_ge(s_r, n + 1)
                    for q in range(2):
                        for a in range(2):
                            half = slice(q * C, (q + 1) * C)
                            src = banks[b][half, 0:NC].rearrange("p (b w a) -> p b w a", b=BC, a=2)[:, :, :, a]
                            scl = rstd[half, b].rearrange("p (b w a) -> p b w a", b=BC, a=2)[:, :, :, a]
                            last = nc.vector.tensor_tensor(rows[a * C:(a + 1) * C, 2 * j + q, c * BC:(c + 1) * BC],
                                                           src, scl, ALU.mult)
                    last.then_inc(s_xn, 1)

            for g in range(G):
                dve.wait_ge(s_h[g], 1)
                nc.vector.tensor_tensor(carry[:, 1, g, :, 1:WP + 1], rows[:, 0, g * BG:(g + 1) * BG],
                                        carry[:, 0, g, :, 1:WP + 1].bitcast(F32),
                                        ALU.subtract).then_inc(s_l[g], 1)

            with dve.Fori(1, H) as t:
                for g in range(G):
                    row = rows[:, t, g * BG:(g + 1) * BG]
                    conv = banks[g][:, 0:NV].rearrange("p (b w) -> p b w", b=BG)
                    dve.wait_ge(s_mm[g], t)
                    nc.vector.scalar_tensor_tensor(row, conv, 0.0, row, ALU.max, ALU.add).then_inc(s_new[g], 1)
                    dve.wait_ge(s_h[g], t + 1)
                    nc.vector.tensor_tensor(carry[:, 1, g, :, 1:WP + 1], row,
                                            carry[:, 0, g, :, 1:WP + 1].bitcast(F32),
                                            ALU.subtract).then_inc(s_l[g], 1)

            def up_step(t, h, par, q):
                for g in range(G):
                    row = rows[:, h, g * BG:(g + 1) * BG].rearrange("p b w -> p (b w)")
                    dve.wait_ge(s_mm[g], t)
                    nc.vector.scalar_tensor_tensor(new_row[:, par, q, g], banks[g][:, 0:NV], 0.0, row,
                                                   ALU.max, ALU.add).then_inc(s_new[g], 1)
                    dve.wait_ge(s_h[g], t + 1)
                    nc.vector.tensor_tensor(carry[:, 1, g, :, 1:WP + 1],
                                            new_row[:, par, q, g].rearrange("p (b w) -> p b w", b=BG),
                                            carry[:, 0, g, :, 1:WP + 1].bitcast(F32), ALU.subtract).then_inc(s_l[g], 1)

            def move_same(j, par):
                for g in range(G):
                    for q in range(2):
                        half = slice(q * C, (q + 1) * C)
                        dst = cols[half, j, g * BG:(g + 1) * BG].rearrange("p b (w a) -> p b w a", a=2)[:, :, :, q]
                        src = new_row[half, par, q, g].rearrange("p (b w) -> p b w", b=BG)
                        nc.vector.tensor_copy(dst, src).then_inc(s_trv, 1)

            PM = 2 * G
            for g in range(G):
                nc.vector.tensor_copy(new_row[:, 1, 1, g].rearrange("p (b w) -> p b w", b=BG),
                                      rows[:, H - 1, g * BG:(g + 1) * BG]).then_inc(s_trv, 1)
            up_step(H, H - 2, 1, 0)
            dve.wait_ge(s_trv, G)
            move_same(HP - 1, 1)
            with dve.Fori(0, (HP - 2) // 2) as i:
                h_odd = [i * -4 + (H - 3 - 2 * par) for par in range(2)]
                h_even = [i * -4 + (H - 4 - 2 * par) for par in range(2)]
                for par in range(2):
                    t = 4 * i + 2 * par + H + 1
                    if par == 1:
                        dve.wait_ge(s_tra, PM * (2 * i + 1) + 1)
                    else:
                        dve.wait_ge(s_tra, PM * 2 * i + 1)
                    up_step(t, h_odd[par], par, 1)
                    up_step(t + 1, h_even[par], par, 0)
                    move_same(HP - 2 - par - 2 * i, par)
            dve.wait_ge(s_tra, PM * (HP - 2) + 1)
            up_step(2 * H - 3, 1, 0, 1)
            for g in range(G):
                nc.vector.tensor_copy(new_row[:, 0, 0, g].rearrange("p (b w) -> p b w", b=BG),
                                      rows[:, 0, g * BG:(g + 1) * BG]).then_inc(s_new[g], 1)
            for g in range(G):
                dve.wait_ge(s_new[g], 2 * H - 2)
            move_same(0, 0)

            dve.wait_ge(s_tra, PM * HP + 1)
            dve.wait_ge(s_trv, G + PM * HP)
            for g in range(G):
                nc.vector.tensor_copy(kbuf[:, g], cols[:, :, g * BG:(g + 1) * BG, 0]).then_inc(s_k[g], 1)

            def col_step(u, w):
                for g in range(G):
                    dve.wait_ge(s_hm[g], u)
                    dve.wait_ge(s_cb[g], u)
                    nc.vector.scalar_tensor_tensor(kbuf[:, g], banks[g][:, 0:NH].rearrange("p (j b) -> p j b", j=HP), 0.0,
                                                   cols[:, :, g * BG:(g + 1) * BG, w], ALU.max, ALU.add).then_inc(s_k[g], 1)

            with dve.Fori(1, W) as u:
                col_step(u, u)
            with dve.Fori(W, 2 * W - 2) as u:
                w = u * -1 + (2 * W - 2)
                col_step(u, w)

            for g in range(G):
                dve.wait_ge(s_cb[g], 2 * W - 2)

            def flat(j):
                return cols[:, j].rearrange("p b w -> p (b w)")

            def residual(j, slot, c):
                t = cols[:, j, c * BC:(c + 1) * BC]
                nc.vector.tensor_tensor(t, t, x_in[:, slot, c * BC:(c + 1) * BC], ALU.add).then_inc(s_t, 1)

            def normalise(j, c):
                n = CH * j + c
                dve.wait_ge(s_r2, n + 1)
                if c > 0:
                    dve.wait_ge(s_tl, n)
                nc.vector.tensor_tensor(xn[:, 0], banks[0][:, 0:NC], rstd[:, 0], ALU.mult).then_inc(s_xn2, 1)

            def second_part(j, slot, c):
                dve.wait_ge(s_th, CH * j + c + 1)
                nc.vector.scalar_tensor_tensor(tok[:, slot, 1, c * NC:(c + 1) * NC], xn[:, 0], 1.0,
                                               tok[:, slot, 0, c * NC:(c + 1) * NC].bitcast(F32),
                                               ALU.add, ALU.subtract).then_inc(s_tl, 1)

            def spread(v):
                return v.unsqueeze(2).to_broadcast([P, NG, E])

            m1, m2, gap, ex, den, idx = (best[:, k] for k in range(6))

            def softmax_steps(j, slot):
                v = nc.vector
                return [
                    lambda: v.tensor_copy(logit, banks[3][:, 0:NSM].rearrange("p (n e) -> p n e", e=E)),
                    lambda: v.tensor_reduce(m1, logit, AX.X, ALU.max),
                    lambda: v.tensor_tensor(hit, logit, spread(m1), ALU.is_equal),
                    lambda: v.tensor_tensor(hit, hit, rank_w[:, :, :], ALU.mult),
                    lambda: v.tensor_reduce(idx, hit, AX.X, ALU.max),
                    lambda: v.tensor_tensor(first, rank_w[:, :, :], spread(idx), ALU.is_equal),
                    lambda: v.scalar_tensor_tensor(rest, first, -BIG, logit, ALU.mult, ALU.add),
                    lambda: v.tensor_reduce(m2, rest, AX.X, ALU.max),
                    lambda: v.tensor_tensor(hit, rest, spread(m2), ALU.is_equal),
                    lambda: v.tensor_tensor(hit, hit, rank_w[:, :, :], ALU.mult),
                    lambda: v.tensor_reduce(idx, hit, AX.X, ALU.max),
                    lambda: v.tensor_tensor(gap, m2, m1, ALU.subtract),
                    lambda: v.tensor_tensor(second, rank_w[:, :, :], spread(idx), ALU.is_equal),
                    lambda: v.tensor_scalar(den, ex, 1.0, None, ALU.add),
                    lambda: v.reciprocal(m1, den),
                    lambda: v.tensor_tensor(gate1, first, spread(m1), ALU.mult),
                    lambda: v.scalar_tensor_tensor(gate2, second, 1.0, spread(ex), ALU.mult, ALU.mult),
                    lambda: v.tensor_tensor(gate2, gate2, spread(m1), ALU.mult),
                    lambda: v.tensor_tensor(gate[slot], gate1, gate2, ALU.add),
                ]

            def softmax(j, slot, lo, hi):
                steps = softmax_steps(j, slot)
                for k in range(lo, hi):
                    if k == 0:
                        dve.wait_ge(s_lt, j + 1)
                    elif k == 13:
                        dve.wait_ge(s_ex, j + 1)
                    if k > 0:
                        dve.wait_ge(s_sm, SMN * j + k)
                    steps[k]().then_inc(s_sm, 1)

            def gate_tile(j, slot, p):
                n, par = TILES * j + p, (TILES * slot + p) % 2
                if p == 0:
                    dve.wait_ge(s_sm, SMN * (j + 1))
                for q in range(2):
                    dve.wait_ge(s_p, 2 * n + q + 1)
                    src = banks[4 + q][:, 0:E * C].rearrange("p (e c) -> p e c", e=E)
                    scl = gate[slot][:, 2 * p + q].unsqueeze(2).to_broadcast([P, E, C])
                    nc.vector.tensor_tensor(gated[:, par, :, q * C:(q + 1) * C], src, scl, ALU.mult).then_inc(s_g, 1)

            def add_out(j, slot, p):
                n, par = TILES * j + p, (TILES * slot + p) % 2
                width, off = (TN, 0) if p < TILES - 1 else (TAIL, TN - TAIL)
                dst = flat(j)[:, p * TN:p * TN + width]
                dve.wait_ge(s_y, n + 1)
                nc.vector.tensor_tensor(dst, banks[6 + par][:, off:off + width], dst, ALU.add).then_inc(s_o, 1)

            def region(j, slot, tiles, tokens, nj, nslot, visit):
                for p in range(TILES):
                    if tokens:
                        if p == 0:
                            dve.wait_ge(s_x[nslot], 32 * (HP // 2 + visit))
                            residual(nj, nslot, 0)
                        if p in (2, 4, 6, 8):
                            normalise(nj, p // 2 - 1)
                    if tiles:
                        gate_tile(j, slot, p)
                        if p >= 1:
                            add_out(j, slot, p - 1)
                    if tokens:
                        if p in (1, 3, 5):
                            residual(nj, nslot, p // 2 + 1)
                        if p in (2, 4, 6, 8):
                            second_part(nj, nslot, p // 2 - 1)
                        if p >= TILES - 3:
                            k = p - (TILES - 3)
                            softmax(nj, nslot, (0, 6, 13)[k], (6, 13, SMN)[k])
                if tiles:
                    add_out(j, slot, TILES - 1)

            region(None, None, False, True, 0, 0, 1)
            region(0, 0, True, True, 1, 1, 1)
            with dve.Fori(1, HP // 2) as i:
                region(2 * i - 1, 1, True, True, 2 * i, 0, i + 1)
                region(2 * i, 0, True, True, 2 * i + 1, 1, i + 1)
            region(HP - 1, 1, True, False, None, None, None)

        @block.tensor
        def _(pe):
            mm = nc.tensor.matmul

            pe.wait_ge(s_id, 1)
            for n in range(8):
                k = n // 2
                shifts = list(enumerate(SHIFTS))[0:4] if n % 2 == 0 else list(enumerate(SHIFTS))[4:SH]
                pe.wait_ge(s_tape, 2 * k + 2)
                for si, s in shifts:
                    t = 2 * s + TAPS // 2
                    taps = tape[:, k, t:t + 2].rearrange("p a c -> p (a c)")
                    last = nc.tensor.transpose(banks[n][:, (si % 4) * P:(si % 4 + 1) * P], taps, ident[:, :])
                last.then_inc(s_wt, 1)

            pe.wait_ge(s_eraw, 6 * 16)
            pe.wait_ge(s_wh, 4)
            pe.wait_ge(s_wv, 4)
            pe.wait_ge(s_cst, NCST)
            mm(banks[0][:, 0:E * C], mean_w[:, :], ew[:, 0:E * C], start=True, stop=True)
            mm(banks[1][:, 0:E], mean_w[:, :], ew[:, E * C:], start=True, stop=True).then_inc(s_cmean, 1)
            pe.wait_ge(s_em, 9)
            pe.wait_ge(s_wh, 8)
            pe.wait_ge(s_cst, NCST)

            def center(n, k):
                slot = k // CH
                if k % CH == 0:
                    pe.wait_ge(s_x[slot], X_COUNT[0])
                pe.wait_ge(s_xn, n + 1)
                c = k % CH
                mm(banks[k % 2][:, 0:NC], center_w[:, :],
                   x_in[:, slot, c * BC:(c + 1) * BC].rearrange("p b w -> p (b w)"),
                   start=True, stop=True).then_inc(s_d, 1)

            def variance(n, k):
                pe.wait_ge(s_sq, n + 1)
                mm(banks[2 + k % 2][:, 0:NC], mean_w[:, :], sq[:, k % 2], start=True, stop=True).then_inc(s_v, 1)

            X_COUNT = [None]
            with pe.Fori(0, HP // 2) as i:
                X_COUNT[0] = 32 * i + 32
                for k in range(2 * CH + 1):
                    if k < 2 * CH:
                        center(2 * CH * i + k, k)
                    if k >= 1:
                        variance(2 * CH * i + k - 1, k - 1)

            def row_step(t, k):
                for g in range(G):
                    acc = banks[g][:, 0:NV].rearrange("p (b w) -> p b w", b=BG)

                    def taps(wpart, cpart, first, final):
                        for si, s in enumerate(SHIFTS):
                            lo, hi = (max(0, -s), min(WP, WP - s)) if abs(s) != 1 else (0, WP)
                            last = mm(acc[:, :, lo:hi], vw[:, k, wpart, si], carry[:, cpart, g, :, lo + s + 1:hi + s + 1],
                                      start=first and si == 0, stop=final and si == SH - 1)
                        return last

                    pe.wait_ge(s_h[g], t)
                    taps(0, 0, True, False)
                    taps(1, 0, False, False)
                    pe.wait_ge(s_l[g], t)
                    taps(0, 1, False, True).then_inc(s_mm[g], 1)

            with pe.Fori(1, H) as t:
                row_step(t, 0)
            with pe.Fori(H, 2 * H - 2) as t:
                row_step(t, 1)

            def col_step(u, k):
                for g in range(G):
                    pe.wait_ge(s_k[g], u)
                    for si, s in enumerate(SHIFTS):
                        lo, hi = max(0, -s), min(HP, HP - s)
                        last = mm(banks[g][:, lo * BG:hi * BG], hw[:, k, si],
                                  kbuf[:, g, lo + s:hi + s].rearrange("p j b -> p (j b)"),
                                  start=si == 0, stop=si == SH - 1)
                    last.then_inc(s_hm[g], 1)

            with pe.Fori(1, W) as u:
                col_step(u, 0)
            with pe.Fori(W, 2 * W - 2) as u:
                col_step(u, 1)

            def center_tokens(j, c):
                n = CH * j + c
                pe.wait_ge(s_t, n + 1)
                pe.wait_ge(s_xn2, n)
                mm(banks[0][:, 0:NC], center_w[:, :],
                   cols[:, j, c * BC:(c + 1) * BC].rearrange("p b w -> p (b w)"),
                   start=True, stop=True).then_inc(s_d2, 1)

            def variance_tokens(j, c):
                n = CH * j + c
                pe.wait_ge(s_sq2, n + 1)
                pe.wait_ge(s_ln2, n)
                mm(banks[1][:, 0:NC], mean_w[:, :], sq[:, 0], start=True, stop=True).then_inc(s_v2, 1)

            def logits(j, slot, c):
                n = CH * j + c
                pe.wait_ge(s_tl, n + 1)
                pe.wait_ge(s_lc, n)
                span = slice(c * NC, (c + 1) * NC)
                mm(banks[2][:, 0:NC], rm[:, 0], tok[:, slot, 0, span], start=True, stop=False)
                mm(banks[2][:, 0:NC], rm[:, 1], tok[:, slot, 0, span], start=False, stop=False)
                mm(banks[2][:, 0:NC], rm[:, 0], tok[:, slot, 1, span], start=False, stop=True).then_inc(s_lg, 1)

            def tile_lo(p):
                return min(p * TN, REG - TN)

            def turn_logits(j, first):
                pe.wait_ge(s_lc, CH * (j + 1))
                if not first:
                    pe.wait_ge(s_sm, SMN * (j - 1) + 1)
                for p in range(TILES):
                    last = mm(banks[3][:, 2 * E * p:2 * E * (p + 1)], logit_c[:, tile_lo(p):tile_lo(p) + TN],
                              ident[0:2 * E, 0:2 * E], start=True, stop=True)
                last.then_inc(s_lt, 1)

            def experts(j, slot, p):
                n = TILES * j + p
                for q in range(2):
                    half, span = slice(q * C, (q + 1) * C), slice(tile_lo(p), tile_lo(p) + TN)
                    pe.wait_ge(s_g, 2 * n + q + 1)
                    for a, b in ((0, 0), (0, 1), (1, 0)):
                        last = mm(banks[4 + q][:, 0:E * C], tok[half, slot, a, span], em[half, b],
                                  start=(a, b) == (0, 0), stop=(a, b) == (1, 0))
                    last.then_inc(s_p, 1)

            def sum_experts(j, slot, p):
                n, par = TILES * j + p, (TILES * slot + p) % 2
                pe.wait_ge(s_g, 2 * n + 4)
                pe.wait_ge(s_o, n + 1)
                for e in range(E):
                    last = mm(banks[6 + par][:, 0:TN], gated[:, par, e], ident[:, :],
                              start=e == 0, stop=e == E - 1, is_transpose=True)
                last.then_inc(s_y, 1)

            def region(j, slot, tiles, tokens, nj, nslot, first):
                for p in range(TILES):
                    if tiles:
                        experts(j, slot, p)
                        if p >= 1:
                            sum_experts(j, slot, p - 1)
                    if tokens:
                        if p in (3, 5, 7, 9):
                            logits(nj, nslot, p // 2 - 1)
                        if p in (0, 2, 4, 6):
                            center_tokens(nj, p // 2)
                        if p in (1, 3, 5, 7):
                            variance_tokens(nj, p // 2)
                        if p == 10:
                            turn_logits(nj, first)
                if tiles:
                    sum_experts(j, slot, TILES - 1)

            region(None, None, False, True, 0, 0, True)
            region(0, 0, True, True, 1, 1, False)
            with pe.Fori(1, HP // 2) as i:
                region(2 * i - 1, 1, True, True, 2 * i, 0, False)
                region(2 * i, 0, True, True, 2 * i + 1, 1, False)
            region(HP - 1, 1, True, False, None, None, False)


_INS = ['x', 'L0_conv_w_d', 'L0_conv_w_u', 'L0_conv_w_r', 'L0_conv_w_l',
        'L0_ffn_router_w', 'L0_ffn_router_b', 'L0_ffn_expert_w', 'L0_ffn_expert_b']


def kernel(**inputs):
    import numpy as np
    import concourse.bacc as bacc
    from concourse.bass_utils import run_bass_kernel_spmd

    nc = bacc.Bacc("TRN2", target_bir_lowering=False, num_devices=1)
    arrays, args = {}, []
    for name in _INS:
        a = np.ascontiguousarray(inputs[name])
        arrays[name] = a
        args.append(nc.dram_tensor(name, a.shape, mybir.dt.from_np(a.dtype), kind="ExternalInput").ap())
    shape = arrays['x'].shape
    args.append(nc.dram_tensor("result", shape, F32, kind="ExternalOutput").ap())
    metaformer_kernel(nc, *args)
    r = run_bass_kernel_spmd(nc, [arrays], core_ids=[0])
    return r.results[0]["result"]
```

```python
from contextlib import ExitStack

import concourse.bass as bass
from concourse import mybir

F32 = mybir.dt.float32
F32R = mybir.dt.float32r
ALU = mybir.AluOpType
ACT = mybir.ActivationFunctionType
AX = mybir.AxisListType


def metaformer_kernel(nc, x, w_d, w_u, w_r, w_l, router_w, router_b, expert_w, expert_b, out):
    B, C, H, W = x.shape
    TAPS = w_d.shape[-1]
    E = expert_w.shape[0]
    P = 2 * C
    HP, WP = H // 2, W // 2
    SH = TAPS // 2 + 1
    SHIFTS = [0, -1, 1, -2, 2]
    TAPE = TAPS + 1
    G = 2
    BG = B // G
    REG = B * W
    NV, NH = BG * WP, HP * BG
    CH = 4
    BC = B // CH
    NC = REG // CH
    TN = 128
    TILES = -(-REG // TN)
    TAIL = REG - (TILES - 1) * TN
    NG = TILES * 2
    BIG = 1.0e30

    ctx = ExitStack()
    with ctx:
        def sb(name, shape, dt=F32):
            return ctx.enter_context(nc.sbuf_tensor(name, shape, dt))

        def sem(name):
            return ctx.enter_context(nc.semaphore(name))

        act_buf = sb("act_buf", [P, HP * REG])
        rows = act_buf[:, :].rearrange("p (h b w) -> p h b w", h=H, b=B)
        cols = act_buf[:, :].rearrange("p (j b w) -> p j b w", j=HP, b=B)
        x_in = sb("x_in", [P, 2, B, W])
        parts = sb("parts", [P, 2 * 2 * REG], F32R)
        nwv = SH * P
        vw = parts[:, 0:4 * nwv].rearrange("p (k l s m) -> p k l s m", k=2, l=2, s=SH)
        NPAD = BG * (WP + 2)
        carry = parts[:, 4 * nwv:4 * nwv + 2 * G * NPAD].rearrange("p (l g b w) -> p l g b w", l=2, g=G, b=BG)
        tok = parts[:, :].rearrange("p (s q n) -> p s q n", s=2, q=2)
        NSM = NG * E
        scratch = sb("scratch", [P, 2 * E * P + 9 * NSM])
        raw_w = scratch[:, 0:4 * C * TAPS].rearrange("p (k n) -> p k n", k=4)
        tape = act_buf[:, (HP * REG - 4 * C * TAPE):].rearrange("p (k t c) -> p k t c", k=4, t=TAPE)
        new_row = scratch[:, 0:2 * 2 * G * NV].rearrange("p (a q g n) -> p a q g n", a=2, q=2, g=G)
        sm = scratch[:, 2 * E * P:].rearrange("p (k n e) -> p k n e", k=9, e=E)
        logit, hit, first, rest, second, gate1, gate2 = (sm[:, k] for k in range(7))
        gate = [sm[:, 7], sm[:, 8]]
        late = sb("late", [P, SH * 2 * P])
        hw = late[:, 0:2 * nwv].rearrange("p (k s m) -> p k s m", k=2, s=SH)
        more = sb("more", [P, E * P])
        gated = [scratch[:, 0:E * P], scratch[:, E * P:2 * E * P], late[:, 0:E * P], more[:, :]]
        gated = [g.rearrange("p (e m) -> p e m", e=E) for g in gated]
        early = act_buf[:, (HP - 8) * REG:(HP - 8) * REG + 3 * 4 * NC].rearrange("p (k b n) -> p k b n", k=3, b=4)
        kbuf = sb("kbuf", [P, G, HP, BG])
        sq = sb("sq", [P, 2, NC])
        lnv = sb("lnv", [P, 2, NC])
        rstd = sb("rstd", [P, 2, NC])
        xn = sb("xn", [P, 1, NC])
        ident = sb("ident", [P, P])
        mean_w = sb("mean_w", [P, P])
        center_w = sb("center_w", [P, P])
        eps_c = sb("eps_c", [P, 2])
        rank_w = sb("rank_w", [P, NG, E])
        ew = sb("ew", [P, E * C + E])
        eb = sb("eb", [P, E * C + E])
        em = sb("em", [P, 2, E * C], F32R)
        rm = sb("rm", [P, 2, E], F32R)
        best = sb("best", [P, 6, NG])

        banks = [ctx.enter_context(nc.psum_tensor(f"bank{i}", [P, 512], F32)) for i in range(8)]

        CONV = [0, 1]
        CEN, VAR = [2, 3], [4, 5]
        OUTS = [[0, 1], [2, 3]]
        TLN = [4, 5]
        LOG = TLN[0]
        SUM = [6, 7]
        ACT_TILES = (0, 2, 4, 6, 7, 8, 9, 11)
        LAG = 2
        SEQ = 2 * TILES

        def gates(engine, j, p, q):
            mine = [(a, b) for a in range(TILES) for b in range(2) if (a in ACT_TILES and b == 1) == (engine == "act")]
            return len(mine) * j + sum(m <= (p, q) for m in mine)

        def stage_of(k):
            k = k % SEQ
            return k % 4 if k < SEQ - 6 else (k - (SEQ - 6)) % 3

        def stage(slot, p):
            return gated[stage_of(TILES * slot + p)]

        def stage_age(slot, p):
            k = TILES * slot + p
            return next(d for d in range(1, SEQ) if stage_of(k - d) == stage_of(k))

        def later(n):
            return not isinstance(n, int) or n > 0


        s_wraw_v = sem("s_wraw_v")
        s_wraw_h = sem("s_wraw_h")
        s_eraw = sem("s_eraw")
        s_x = [sem("s_x0"), sem("s_x1")]
        s_id0 = sem("s_id0")
        s_id = sem("s_id")
        s_cst = sem("s_cst")
        s_tape0 = sem("s_tape0")
        s_tape = sem("s_tape")
        s_wt = sem("s_wt")
        s_wh = sem("s_wh")
        s_wv = sem("s_wv")
        s_cmean = sem("s_cmean")
        s_em = sem("s_em")
        s_d = sem("s_d")
        s_sq = sem("s_sq")
        s_v = sem("s_v")
        s_ln = sem("s_ln")
        s_r = sem("s_r")
        s_xn = sem("s_xn")
        s_h = [sem(f"s_h{g}") for g in range(G)]
        s_l = [sem(f"s_l{g}") for g in range(G)]
        s_mm = [sem(f"s_mm{g}") for g in range(G)]
        s_new = [sem(f"s_new{g}") for g in range(G)]
        s_trv = sem("s_trv")
        s_tra = sem("s_tra")
        s_k = [sem(f"s_k{g}") for g in range(G)]
        s_hm = [sem(f"s_hm{g}") for g in range(G)]
        s_cb = [sem(f"s_cb{g}") for g in range(G)]
        s_t = sem("s_t")
        s_d2 = sem("s_d2")
        s_sq2 = sem("s_sq2")
        s_v2 = sem("s_v2")
        s_ln2 = sem("s_ln2")
        s_r2 = sem("s_r2")
        s_xn2 = sem("s_xn2")
        s_th = sem("s_th")
        s_tl = sem("s_tl")
        s_lt = sem("s_lt")
        s_sm = sem("s_sm")
        s_ex = sem("s_ex")
        s_p = sem("s_p")
        s_g = sem("s_g")
        s_ga = sem("s_ga")
        s_ps = sem("s_ps")
        s_y = sem("s_y")
        s_o = sem("s_o")
        s_out = sem("s_out")

        block = ctx.enter_context(nc.Block())

        def pair_view(dram, j, q):
            return dram.rearrange("b c (j q) w -> q j c b w", q=2)[q, j]

        def load_conv(engine, k, w):
            for q in range(2):
                engine.dma_start(raw_w[q * C:(q + 1) * C, k], w.rearrange("o i a b -> o (i a b)")).then_inc(s_wraw_v if k < 2 else s_wraw_h, 16)

        @block.sync
        def _(sp):
            def load(j, slot):
                for q in range(2):
                    sp.dma_start(x_in[q * C:(q + 1) * C, slot], pair_view(x, j, q)).then_inc(s_x[slot], 16)

            load(0, 0)
            load(1, 1)
            load_conv(sp, 2, w_r)
            load_conv(sp, 3, w_l)
            for q in range(2):
                half = slice(q * C, (q + 1) * C)
                sp.dma_start(ew[half, 0:E * C].rearrange("p (e c) -> p e c", e=E),
                              expert_w.rearrange("e d c -> d e c")).then_inc(s_eraw, 16)
                sp.dma_start(ew[half, E * C:], router_w).then_inc(s_eraw, 16)
            sp.dma_start(eb[:, 0:E * C],
                          expert_b.rearrange("(o e) c -> o (e c)", o=1).broadcast_to([P, E * C])).then_inc(s_eraw, 16)
            sp.dma_start(eb[:, E * C:], router_b.rearrange("(o e) -> o e", o=1).broadcast_to([P, E])).then_inc(s_eraw, 16)
            with sp.Fori(1, HP // 2) as i:
                for slot in range(2):
                    sp.wait_ge(s_d, 2 * CH * i - CH + CH * slot)
                    load(2 * i + slot, slot)
            for slot in range(2):
                sp.wait_ge(s_d, CH * (HP - 1 + slot))
                load(slot, slot)

            def store(j):
                sp.wait_ge(s_o, 2 + TILES * (j + 1))
                for q in range(2):
                    sp.dma_start(pair_view(out, j, q), cols[q * C:(q + 1) * C, j]).then_inc(s_out, 16)

            def reload(j, slot):
                sp.wait_ge(s_t, CH * (j - 1))
                load(j, slot)

            reload(2, 0)
            with sp.Fori(0, HP // 2 - 2) as i:
                for slot in range(2):
                    reload(2 * i + slot + 3, 1 - slot)
                    store(2 * i + slot)
            reload(HP - 1, 1)
            for j in range(HP - 4, HP):
                store(j)
            sp.wait_ge(s_out, HP * 32)

        @block.gpsimd
        def _(pool):
            nc.gpsimd.memset(ident[:, :], 0.0).then_inc(s_id0, 1)
            pool.wait_ge(s_id0, 1)
            nc.gpsimd.affine_select(out=ident[:, :], in_=ident[:, :], compare_op=ALU.not_equal, fill=1.0,
                                    base=0, pattern=[[-1, P]], channel_multiplier=1).then_inc(s_id, 1)

            def residual(j, slot, c):
                t = cols[:, j, c * BC:(c + 1) * BC]
                nc.gpsimd.tensor_tensor(t, t, x_in[:, slot, c * BC:(c + 1) * BC], ALU.add).then_inc(s_t, 1)

            def pair_sums(j, slot, p):
                pool.wait_ge(s_g, gates("dve", j, p, 1))
                if p in ACT_TILES:
                    pool.wait_ge(s_ga, gates("act", j, p, 1))
                buf = stage(slot, p)
                nc.gpsimd.tensor_tensor(buf[:, 0:4], buf[:, 0:4], buf[:, 4:8], ALU.add).then_inc(s_ps, 1)

            def region(j, slot, ahead, visit):
                for p in range(TILES):
                    if ahead is not None and p in (6, 8, 10, 12):
                        if p == 6:
                            pool.wait_ge(s_x[slot], 32 * (HP // 2 + visit))
                        residual(ahead, slot, p // 2 - 3)
                    if j is not None:
                        pair_sums(j, slot, p)

            for g in range(G):
                pool.wait_ge(s_cb[g], 2 * W - 2)
            region(None, 0, 0, 1)
            region(None, 1, 1, 1)
            region(0, 0, 2, 2)
            with pool.Fori(1, HP // 2 - 1) as i:
                region(2 * i - 1, 1, 2 * i + 1, i + 1)
                region(2 * i, 0, 2 * i + 2, i + 2)
            region(HP - 3, 1, HP - 1, HP // 2)
            region(HP - 2, 0, None, None)
            region(HP - 1, 1, None, None)

        SMN = 19
        GAP_STEP = 12
        STEP_AT = [(7, 1), (7, 2), (8, 0), (8, 1), (8, 2), (9, 0), (9, 1), (9, 2), (10, 0), (10, 1), (10, 2),
                   (10, 2), (11, 0), (11, 1), (11, 1), (11, 2), (11, 2), (12, 0), (12, 1)]
        EXP_TILE = STEP_AT[GAP_STEP - 1][0] + 1
        NCST = 4 + E + 2 + 1

        @block.scalar
        def _(act):
            load_conv(act, 0, w_d)
            load_conv(act, 1, w_u)
            nc.scalar.preload_act_table_set("natural_log_exp_and_others")
            def square(n, b):
                act.wait_ge(s_d, n + 1)
                act.activation(sq[:, b], banks[CEN[b]][:, 0:NC], ACT.Square).then_inc(s_sq, 1)

            def inv_std(n, b):
                act.wait_ge(s_v, n + 1)
                act.wait_ge(s_xn, n + 1)
                act.activation(lnv[:, b], banks[VAR[b]][:, 0:NC], ACT.Ln, bias=eps_c[:, 0:1]).then_inc(s_ln, 1)
                act.wait_ge(s_ln, n + 1)
                act.activation(rstd[:, b], lnv[:, b], ACT.Exp, scale=-0.5).then_inc(s_r, 1)

            act.wait_ge(s_cst, NCST)
            for k in range(2 * CH + 2):
                if k < 2 * CH:
                    act.wait_ge(s_d, k + 1)
                    act.activation(early[:, 0, k % 4], banks[k % 4][:, 0:NC], ACT.Square).then_inc(s_sq, 1)
                if k >= 2:
                    act.wait_ge(s_v, k - 1)
                    if k >= 6:
                        act.wait_ge(s_xn, k - 3)
                    act.activation(early[:, 1, (k - 2) % 4], banks[4 + (k - 2) % 4][:, 0:NC], ACT.Ln,
                                   bias=eps_c[:, 0:1]).then_inc(s_ln, 1)
                    act.wait_ge(s_ln, k - 1)
                    act.activation(early[:, 2, (k - 2) % 4], early[:, 1, (k - 2) % 4], ACT.Exp,
                                   scale=-0.5).then_inc(s_r, 1)
            for n in range(8):
                k = n // 2
                act.wait_ge(s_wt, n + 1)
                lo, hi = (0, 4) if n % 2 == 0 else (4, SH)
                dst = vw[:, k, 0, lo:hi] if k < 2 else hw[:, k - 2, lo:hi]
                act.activation(dst, banks[n][:, 0:(hi - lo) * P].rearrange("p (s m) -> p s m", m=P),
                               ACT.Copy).then_inc(s_wh, 1)

            act.wait_ge(s_xn, 2 + 2 * CH)
            for g in range(G):
                act.activation(carry[:, 0, g, :, 1:WP + 1],
                               rows[:, 0, g * BG:(g + 1) * BG], ACT.Copy).then_inc(s_h[g], 1)

            def down_round(t, g):
                act.wait_ge(s_new[g], t)
                act.activation(carry[:, 0, g, :, 1:WP + 1],
                               rows[:, t, g * BG:(g + 1) * BG], ACT.Copy).then_inc(s_h[g], 1)

            def down_pair(i, norm):
                for m in range(CH):
                    if norm:
                        square(CH * (i + 2) + m, m % 2)
                    down_round(2 * i + 1 + m // G, m % G)
                    if norm:
                        inv_std(CH * (i + 2) + m, m % 2)

            with act.Fori(0, (HP - 2) // 2) as i:
                for u in range(2):
                    down_pair(2 * i + u, True)
            down_pair(HP - 2, False)
            for g in range(G):
                down_round(H - 1, g)

            def round_row(t, par, q):
                for g in range(G):
                    act.wait_ge(s_new[g], t)
                    act.activation(carry[:, 0, g, :, 1:WP + 1],
                                   new_row[:, par, q, g].rearrange("p (b w) -> p b w", b=BG), ACT.Copy).then_inc(s_h[g], 1)

            def move_cross(j, par):
                for g in range(G):
                    for q in range(2):
                        dst = cols[q * C:(q + 1) * C, j, g * BG:(g + 1) * BG].rearrange("p b (w a) -> p b w a", a=2)[:, :, :, 1 - q]
                        src = new_row[(1 - q) * C:(2 - q) * C, par, q, g].rearrange("p (b w) -> p b w", b=BG)
                        act.activation(dst, src, ACT.Copy).then_inc(s_tra, 1)

            round_row(H, 1, 0)
            act.wait_ge(s_trv, G)
            move_cross(HP - 1, 1)
            with act.Fori(0, (HP - 2) // 2) as i:
                for par in range(2):
                    t = 4 * i + 2 * par + H + 1
                    round_row(t, par, 1)
                    round_row(t + 1, par, 0)
                    move_cross(HP - 2 - par - 2 * i, par)
            round_row(2 * H - 3, 0, 1)
            for g in range(G):
                act.wait_ge(s_new[g], 2 * H - 2)
            move_cross(0, 0)

            def copy_back(u, w):
                for g in range(G):
                    act.wait_ge(s_k[g], u + 1)
                    act.activation(cols[:, :, g * BG:(g + 1) * BG, w], kbuf[:, g], ACT.Copy).then_inc(s_cb[g], 1)

            with act.Fori(1, W) as u:
                copy_back(u, u)
            with act.Fori(W, 2 * W - 2) as u:
                w = u * -1 + (2 * W - 2)
                copy_back(u, w)

            def norm_square(j, c):
                act.wait_ge(s_d2, CH * j + c + 1)
                act.activation(sq[:, c % 2], banks[TLN[c % 2]][:, 0:NC], ACT.Square).then_inc(s_sq2, 1)

            def norm_std(j, c):
                n = CH * j + c
                act.wait_ge(s_v2, n + 1)
                act.activation(lnv[:, c % 2], banks[TLN[1 - c % 2]][:, 0:NC], ACT.Ln, bias=eps_c[:, 1:2]).then_inc(s_ln2, 1)
                act.wait_ge(s_ln2, n + 1)
                act.activation(rstd[:, c % 2], lnv[:, c % 2], ACT.Exp, scale=-0.5).then_inc(s_r2, 1)

            def first_part(j, slot, c):
                act.wait_ge(s_xn2, CH * j + c + 1)
                if c == 0 and later(j - 1):
                    act.wait_ge(s_p, 2 * TILES * (j - 1))
                for q in range(2):
                    half = slice(q * C, (q + 1) * C)
                    act.activation(tok[half, slot, q, c * NC:(c + 1) * NC], xn[half, 0], ACT.Identity,
                                   bias=1.0).then_inc(s_th, 1)

            def exponential(j):
                act.wait_ge(s_sm, SMN * j + GAP_STEP)
                act.activation(best[:, 3], best[:, 2], ACT.Exp).then_inc(s_ex, 1)

            def gate_odd(j, slot, p):
                n = TILES * j + p
                act.wait_ge(s_sm, SMN * (j + 1))
                if later(n - stage_age(slot, p) + 1):
                    act.wait_ge(s_y, n - stage_age(slot, p) + 1)
                act.wait_ge(s_p, 2 * n + 2)
                for e in range(E):
                    last = act.activation(stage(slot, p)[:, e, C:P], banks[OUTS[(TILES * slot + p) % 2][1]][:, e * C:(e + 1) * C],
                                          ACT.Copy, scale=gate[slot][:, 2 * p + 1, e:e + 1])
                last.then_inc(s_ga, 1)

            def region(j, slot, now, ahead):
                for p in range(TILES):
                    if now is not None:
                        if p in (0, 2, 4):
                            first_part(now, 1 - slot, p // 2 + 1)
                        if p in (0, 2):
                            norm_square(now, p // 2 + 2)
                        if p in (1, 3):
                            norm_std(now, (p + 3) // 2)
                        if p == EXP_TILE:
                            exponential(now)
                    if ahead is not None:
                        if p == 9:
                            norm_square(ahead, 0)
                        if p == 10:
                            norm_std(ahead, 0)
                        if p == 11:
                            first_part(ahead, slot, 0)
                            norm_square(ahead, 1)
                        if p == 12:
                            norm_std(ahead, 1)
                    if j is not None and p in ACT_TILES:
                        gate_odd(j, slot, p)

            region(None, 0, None, 0)
            region(None, 1, 0, 1)
            region(0, 0, 1, 2)
            with act.Fori(1, HP // 2 - 1) as i:
                region(2 * i - 1, 1, 2 * i, 2 * i + 1)
                region(2 * i, 0, 2 * i + 1, 2 * i + 2)
            region(HP - 3, 1, HP - 2, HP - 1)
            region(HP - 2, 0, HP - 1, None)
            region(HP - 1, 1, None, None)

        @block.vector
        def _(dve):
            nc.vector.memset(best[:, :, :], 0.0).then_inc(s_xn, 2)
            for edge in (0, WP + 1):
                for k in range(2):
                    nc.vector.memset(carry[:, k, :, :, edge].bitcast(F32), 0.0).then_inc(s_tape0, 1)
            for q in range(2):
                nc.vector.memset(tape[q * C:(q + 1) * C, :, (1 - q) * TAPS], 0.0).then_inc(s_tape0, 1)
            nc.vector.memset(lnv[:, 0, 0:1], 0.0).then_inc(s_o, 2)
            nc.vector.memset(lnv[:, 0, 1:2], 0.0).then_inc(s_tra, 1)
            for g in range(G):
                nc.vector.memset(lnv[:, 1, g:g + 1], 0.0).then_inc(s_cb[g], 1)
            for q in range(2):
                for a in range(2):
                    nc.vector.memset(mean_w[q * C:(q + 1) * C, a * C:(a + 1) * C],
                                     1.0 / C if a == q else 0.0).then_inc(s_cst, 1)
            for e in range(E):
                nc.vector.memset(rank_w[:, :, e], float(E - e)).then_inc(s_cst, 1)
            nc.vector.memset(eps_c[:, 0:1], 1.0e-6).then_inc(s_cst, 1)
            nc.vector.memset(eps_c[:, 1:2], 1.0e-5).then_inc(s_cst, 1)
            dve.wait_ge(s_id, 1)
            dve.wait_ge(s_cst, 4)
            nc.vector.tensor_tensor(center_w[:, :], ident[:, :], mean_w[:, :], ALU.subtract).then_inc(s_cst, 1)
            dve.wait_ge(s_wraw_v, 4 * 16)
            dve.wait_ge(s_tape0, 6)
            def space_taps(k):
                for q in range(2):
                    nc.vector.tensor_copy(tape[q * C:(q + 1) * C, k, q:q + TAPS],
                                          raw_w[q * C:(q + 1) * C, k].rearrange("p (c t) -> p t c", t=TAPS)).then_inc(s_tape, 1)

            space_taps(0)
            space_taps(1)
            def normalise_rows(n, b, j, c, centred=None, inv=None):
                if centred is None:
                    centred, inv = banks[CEN[b]][:, 0:NC], rstd[:, b]
                dve.wait_ge(s_r, n + 1)
                for q in range(2):
                    for a in range(2):
                        half = slice(q * C, (q + 1) * C)
                        src = centred[half].rearrange("p (b w a) -> p b w a", b=BC, a=2)[:, :, :, a]
                        scl = inv[half].rearrange("p (b w a) -> p b w a", b=BC, a=2)[:, :, :, a]
                        last = nc.vector.tensor_tensor(rows[a * C:(a + 1) * C, 2 * j + q, c * BC:(c + 1) * BC],
                                                       src, scl, ALU.mult)
                last.then_inc(s_xn, 1)

            for k in range(2 * CH):
                normalise_rows(k, k % 4, k // CH, k % CH, banks[k % 4][:, 0:NC], early[:, 2, k % 4])

            dve.wait_ge(s_wraw_h, 4 * 16)
            space_taps(2)
            space_taps(3)
            for n in range(4):
                lo, hi = (0, 4) if n % 2 == 0 else (4, SH)
                dve.wait_ge(s_wh, n + 1)
                nc.vector.tensor_tensor(vw[:, n // 2, 1, lo:hi], banks[n][:, 0:(hi - lo) * P].rearrange("p (s m) -> p s m", m=P),
                                        vw[:, n // 2, 0, lo:hi].bitcast(F32), ALU.subtract).then_inc(s_wv, 1)
            for g in range(G):
                dve.wait_ge(s_h[g], 1)
                nc.vector.tensor_tensor(carry[:, 1, g, :, 1:WP + 1], rows[:, 0, g * BG:(g + 1) * BG],
                                        carry[:, 0, g, :, 1:WP + 1].bitcast(F32),
                                        ALU.subtract).then_inc(s_l[g], 1)

            dve.wait_ge(s_cmean, 1)
            dve.wait_ge(s_eraw, 6 * 16)
            nc.vector.tensor_tensor(ew[:, 0:E * C], ew[:, 0:E * C], banks[SUM[0]][:, 0:E * C], ALU.subtract).then_inc(s_em, 1)
            nc.vector.tensor_tensor(ew[:, E * C:], ew[:, E * C:], banks[SUM[1]][:, 0:E], ALU.subtract).then_inc(s_em, 1)
            dve.wait_ge(s_em, 2)
            nc.vector.scalar_tensor_tensor(ew[:, :], eb[:, :], 1.0 / C, ew[:, :], ALU.mult, ALU.add).then_inc(s_em, 1)
            dve.wait_ge(s_em, 3)
            nc.vector.tensor_copy(em[:, 0], ew[:, 0:E * C]).then_inc(s_em, 1)
            nc.vector.tensor_copy(rm[:, 0], ew[:, E * C:]).then_inc(s_em, 1)
            dve.wait_ge(s_em, 5)
            nc.vector.tensor_tensor(em[:, 1], ew[:, 0:E * C], em[:, 0].bitcast(F32), ALU.subtract).then_inc(s_em, 1)
            nc.vector.tensor_tensor(rm[:, 1], ew[:, E * C:], rm[:, 0].bitcast(F32), ALU.subtract).then_inc(s_em, 1)

            def down_step(t, g, between):
                row = rows[:, t, g * BG:(g + 1) * BG]
                conv = banks[CONV[g]][:, 0:NV].rearrange("p (b w) -> p b w", b=BG)
                dve.wait_ge(s_mm[g], t)
                nc.vector.scalar_tensor_tensor(row, conv, 0.0, row, ALU.max, ALU.add).then_inc(s_new[g], 1)
                between()
                dve.wait_ge(s_h[g], t + 1)
                nc.vector.tensor_tensor(carry[:, 1, g, :, 1:WP + 1], row,
                                        carry[:, 0, g, :, 1:WP + 1].bitcast(F32), ALU.subtract).then_inc(s_l[g], 1)

            def down_pair(i, before, norm):
                for m in range(CH):
                    def between():
                        if m == 0 and before:
                            normalise_rows(CH * (i + 1) + CH - 1, 1, i + 1, CH - 1)
                        if m > 0 and norm:
                            normalise_rows(CH * (i + 2) + m - 1, (m - 1) % 2, i + 2, m - 1)
                    down_step(2 * i + 1 + m // G, m % G, between)

            down_pair(0, False, True)
            down_pair(1, True, True)
            with dve.Fori(1, (HP - 2) // 2) as i:
                for u in range(2):
                    down_pair(2 * i + u, True, True)
            down_pair(HP - 2, True, False)
            for g in range(G):
                down_step(H - 1, g, lambda: None)

            def up_step(t, h, par, q):
                for g in range(G):
                    row = rows[:, h, g * BG:(g + 1) * BG].rearrange("p b w -> p (b w)")
                    dve.wait_ge(s_mm[g], t)
                    nc.vector.scalar_tensor_tensor(new_row[:, par, q, g], banks[CONV[g]][:, 0:NV], 0.0, row,
                                                   ALU.max, ALU.add).then_inc(s_new[g], 1)
                    dve.wait_ge(s_h[g], t + 1)
                    nc.vector.tensor_tensor(carry[:, 1, g, :, 1:WP + 1],
                                            new_row[:, par, q, g].rearrange("p (b w) -> p b w", b=BG),
                                            carry[:, 0, g, :, 1:WP + 1].bitcast(F32), ALU.subtract).then_inc(s_l[g], 1)

            def move_same(j, par):
                for g in range(G):
                    for q in range(2):
                        half = slice(q * C, (q + 1) * C)
                        dst = cols[half, j, g * BG:(g + 1) * BG].rearrange("p b (w a) -> p b w a", a=2)[:, :, :, q]
                        src = new_row[half, par, q, g].rearrange("p (b w) -> p b w", b=BG)
                        nc.vector.tensor_copy(dst, src).then_inc(s_trv, 1)

            PM = 2 * G
            for g in range(G):
                nc.vector.tensor_copy(new_row[:, 1, 1, g].rearrange("p (b w) -> p b w", b=BG),
                                      rows[:, H - 1, g * BG:(g + 1) * BG]).then_inc(s_trv, 1)
            up_step(H, H - 2, 1, 0)
            dve.wait_ge(s_trv, G)
            move_same(HP - 1, 1)
            with dve.Fori(0, (HP - 2) // 2) as i:
                h_odd = [i * -4 + (H - 3 - 2 * par) for par in range(2)]
                h_even = [i * -4 + (H - 4 - 2 * par) for par in range(2)]
                for par in range(2):
                    t = 4 * i + 2 * par + H + 1
                    if par == 1:
                        dve.wait_ge(s_tra, PM * (2 * i + 1) + 1)
                    else:
                        dve.wait_ge(s_tra, PM * 2 * i + 1)
                    up_step(t, h_odd[par], par, 1)
                    up_step(t + 1, h_even[par], par, 0)
                    move_same(HP - 2 - par - 2 * i, par)
            dve.wait_ge(s_tra, PM * (HP - 2) + 1)
            up_step(2 * H - 3, 1, 0, 1)
            for g in range(G):
                nc.vector.tensor_copy(new_row[:, 0, 0, g].rearrange("p (b w) -> p b w", b=BG),
                                      rows[:, 0, g * BG:(g + 1) * BG]).then_inc(s_new[g], 1)
            for g in range(G):
                dve.wait_ge(s_new[g], 2 * H - 2)
            move_same(0, 0)

            dve.wait_ge(s_tra, PM * HP + 1)
            dve.wait_ge(s_trv, G + PM * HP)
            for g in range(G):
                nc.vector.tensor_copy(kbuf[:, g], cols[:, :, g * BG:(g + 1) * BG, 0]).then_inc(s_k[g], 1)

            def col_step(u, w):
                for g in range(G):
                    dve.wait_ge(s_hm[g], u)
                    dve.wait_ge(s_cb[g], u)
                    nc.vector.scalar_tensor_tensor(kbuf[:, g], banks[CONV[g]][:, 0:NH].rearrange("p (j b) -> p j b", j=HP), 0.0,
                                                   cols[:, :, g * BG:(g + 1) * BG, w], ALU.max, ALU.add).then_inc(s_k[g], 1)

            with dve.Fori(1, W) as u:
                col_step(u, u)
            with dve.Fori(W, 2 * W - 2) as u:
                w = u * -1 + (2 * W - 2)
                col_step(u, w)

            def flat(j):
                return cols[:, j].rearrange("p b w -> p (b w)")

            def normalise(j, c):
                n = CH * j + c
                dve.wait_ge(s_r2, n + 1)
                if later(n):
                    dve.wait_ge(s_tl, 2 * n)
                nc.vector.tensor_tensor(xn[:, 0], banks[TLN[c % 2]][:, 0:NC], rstd[:, c % 2], ALU.mult).then_inc(s_xn2, 1)

            def second_part(j, slot, c):
                dve.wait_ge(s_th, 2 * (CH * j + c + 1))
                span = slice(c * NC, (c + 1) * NC)
                for q in range(2):
                    half, other = slice(q * C, (q + 1) * C), slice((1 - q) * C, (2 - q) * C)
                    nc.vector.scalar_tensor_tensor(tok[other, slot, q, span], xn[half, 0], 1.0,
                                                   tok[half, slot, q, span].bitcast(F32),
                                                   ALU.add, ALU.subtract).then_inc(s_tl, 1)

            def spread(v):
                return v.unsqueeze(2).to_broadcast([P, NG, E])

            m1, m2, gap, ex, den, idx = (best[:, k] for k in range(6))

            def softmax_steps(j, slot):
                v = nc.vector
                return [
                    lambda: v.tensor_reduce(logit, banks[LOG][:, 0:2 * NSM].rearrange("p (n l e) -> p n e l", l=2, e=E), AX.X, ALU.add),
                    lambda: v.tensor_reduce(m1, logit, AX.X, ALU.max),
                    lambda: v.tensor_tensor(hit, logit, spread(m1), ALU.is_equal),
                    lambda: v.tensor_tensor(hit, hit, rank_w[:, :, :], ALU.mult),
                    lambda: v.tensor_reduce(idx, hit, AX.X, ALU.max),
                    lambda: v.tensor_tensor(first, rank_w[:, :, :], spread(idx), ALU.is_equal),
                    lambda: v.scalar_tensor_tensor(rest, first, -BIG, logit, ALU.mult, ALU.add),
                    lambda: v.tensor_reduce(m2, rest, AX.X, ALU.max),
                    lambda: v.tensor_tensor(hit, rest, spread(m2), ALU.is_equal),
                    lambda: v.tensor_tensor(hit, hit, rank_w[:, :, :], ALU.mult),
                    lambda: v.tensor_reduce(idx, hit, AX.X, ALU.max),
                    lambda: v.tensor_tensor(gap, m2, m1, ALU.subtract),
                    lambda: v.tensor_tensor(second, rank_w[:, :, :], spread(idx), ALU.is_equal),
                    lambda: v.tensor_scalar(den, ex, 1.0, None, ALU.add),
                    lambda: v.reciprocal(m1, den),
                    lambda: v.tensor_tensor(m2, ex, m1, ALU.mult),
                    lambda: v.tensor_tensor(gate1, first, spread(m1), ALU.mult),
                    lambda: v.tensor_tensor(gate2, second, spread(m2), ALU.mult),
                    lambda: v.tensor_tensor(gate[slot], gate1, gate2, ALU.add),
                ]

            def softmax(j, slot, at):
                steps = softmax_steps(j, slot)
                for k in range(SMN):
                    if STEP_AT[k] == at:
                        if k == 0:
                            dve.wait_ge(s_lt, j + 1)
                        elif k == GAP_STEP + 1:
                            dve.wait_ge(s_ex, j + 1)
                        if k > 0:
                            dve.wait_ge(s_sm, SMN * j + k)
                        steps[k]().then_inc(s_sm, 1)

            def gate_half(j, slot, p, q):
                n = TILES * j + p
                if q == 0:
                    if p == 0:
                        dve.wait_ge(s_sm, SMN * (j + 1))
                    if later(n - stage_age(slot, p) + 1):
                        dve.wait_ge(s_y, n - stage_age(slot, p) + 1)
                dve.wait_ge(s_p, 2 * n + q + 1)
                src = banks[OUTS[(TILES * slot + p) % 2][q]][:, 0:E * C].rearrange("p (e c) -> p e c", e=E)
                scl = gate[slot][:, 2 * p + q].unsqueeze(2).to_broadcast([P, E, C])
                nc.vector.tensor_tensor(stage(slot, p)[:, :, q * C:(q + 1) * C], src, scl, ALU.mult).then_inc(s_g, 1)

            def add_out(j, slot, p):
                n, par = TILES * j + p, (TILES * slot + p) % 2
                width, off = (TN, 0) if p < TILES - 1 else (TAIL, TN - TAIL)
                dst = flat(j)[:, p * TN:p * TN + width]
                dve.wait_ge(s_y, n + 1)
                nc.vector.tensor_tensor(dst, banks[SUM[par]][:, off:off + width], dst, ALU.add).then_inc(s_o, 1)

            def add_behind(j, slot, p):
                if p >= LAG:
                    add_out(j, slot, p - LAG)
                elif later(j):
                    add_out(j - 1, 1 - slot, TILES + p - LAG)

            def region(j, slot, now, ahead):
                for p in range(TILES):
                    if now is not None and p in (0, 2, 4):
                        normalise(now, p // 2 + 1)
                    if ahead is not None and p == 11:
                        normalise(ahead, 0)
                    for part in range(3):
                        if j is not None:
                            if part == 2:
                                add_behind(j, slot, p)
                            elif part == 0 or p not in ACT_TILES:
                                gate_half(j, slot, p, part)
                        if now is not None:
                            softmax(now, 1 - slot, (p, part))
                    if now is not None and p in (0, 2, 4):
                        second_part(now, 1 - slot, p // 2 + 1)
                    if ahead is not None and p == 11:
                        second_part(ahead, slot, 0)

            region(None, 0, None, 0)
            region(None, 1, 0, 1)
            region(0, 0, 1, 2)
            with dve.Fori(1, HP // 2 - 1) as i:
                region(2 * i - 1, 1, 2 * i, 2 * i + 1)
                region(2 * i, 0, 2 * i + 1, 2 * i + 2)
            region(HP - 3, 1, HP - 2, HP - 1)
            region(HP - 2, 0, HP - 1, None)
            region(HP - 1, 1, None, None)
            for p in range(TILES - LAG, TILES):
                add_out(HP - 1, 1, p)

        @block.tensor
        def _(pe):
            mm = nc.tensor.matmul

            def center(n, b, slot, c):
                pe.wait_ge(s_xn, n + 1)
                mm(banks[CEN[b]][:, 0:NC], center_w[:, :],
                   x_in[:, slot, c * BC:(c + 1) * BC].rearrange("p b w -> p (b w)"),
                   start=True, stop=True).then_inc(s_d, 1)

            def variance(n, b):
                pe.wait_ge(s_sq, n + 1)
                mm(banks[VAR[b]][:, 0:NC], mean_w[:, :], sq[:, b], start=True, stop=True).then_inc(s_v, 1)

            pe.wait_ge(s_id, 1)
            pe.wait_ge(s_cst, NCST)
            for k in range(2 * CH + 1):
                if k < 2 * CH:
                    if k % CH == 0:
                        pe.wait_ge(s_x[k // CH], 32)
                    if k >= 4:
                        pe.wait_ge(s_xn, k - 1)
                    c = k % CH
                    mm(banks[k % 4][:, 0:NC], center_w[:, :],
                       x_in[:, k // CH, c * BC:(c + 1) * BC].rearrange("p b w -> p (b w)"),
                       start=True, stop=True).then_inc(s_d, 1)
                if k >= 1:
                    pe.wait_ge(s_sq, k)
                    mm(banks[4 + (k - 1) % 4][:, 0:NC], mean_w[:, :], early[:, 0, (k - 1) % 4],
                       start=True, stop=True).then_inc(s_v, 1)
            pe.wait_ge(s_xn, 2 + 2 * CH)

            for n in range(8):
                k = n // 2
                shifts = list(enumerate(SHIFTS))[0:4] if n % 2 == 0 else list(enumerate(SHIFTS))[4:SH]
                pe.wait_ge(s_tape, 2 * k + 2)
                for si, s in shifts:
                    t = 2 * s + TAPS // 2
                    taps = tape[:, k, t:t + 2].rearrange("p a c -> p (a c)")
                    last = nc.tensor.transpose(banks[n][:, (si % 4) * P:(si % 4 + 1) * P], taps, ident[:, :])
                last.then_inc(s_wt, 1)

            pe.wait_ge(s_eraw, 6 * 16)
            pe.wait_ge(s_wh, 8)
            pe.wait_ge(s_wv, 4)
            mm(banks[SUM[0]][:, 0:E * C], mean_w[:, :], ew[:, 0:E * C], start=True, stop=True)
            mm(banks[SUM[1]][:, 0:E], mean_w[:, :], ew[:, E * C:], start=True, stop=True).then_inc(s_cmean, 1)

            def row_step(t, k, g, middle=lambda: None):
                acc = banks[CONV[g]][:, 0:NV].rearrange("p (b w) -> p b w", b=BG)

                def taps(wpart, cpart, first, final):
                    for si, s in enumerate(SHIFTS):
                        lo, hi = (max(0, -s), min(WP, WP - s)) if abs(s) != 1 else (0, WP)
                        last = mm(acc[:, :, lo:hi], vw[:, k, wpart, si], carry[:, cpart, g, :, lo + s + 1:hi + s + 1],
                                  start=first and si == 0, stop=final and si == SH - 1)
                    return last

                pe.wait_ge(s_h[g], t)
                taps(0, 0, True, False)
                taps(1, 0, False, False)
                middle()
                pe.wait_ge(s_l[g], t)
                taps(0, 1, False, True).then_inc(s_mm[g], 1)

            def down_pair(i, slot, visit):
                for m in range(CH):
                    n = CH * (i + 2) + m

                    def middle():
                        if m == 0:
                            pe.wait_ge(s_x[slot], 32 * visit)
                        center(n, m % 2, slot, m)
                    row_step(2 * i + 1 + m // G, 0, m % G, middle)
                    variance(n, m % 2)

            with pe.Fori(0, (HP - 2) // 2) as i:
                for u in range(2):
                    down_pair(2 * i + u, u, i + 2)
            for t in range(H - 3, H):
                for g in range(G):
                    row_step(t, 0, g)
            with pe.Fori(H, 2 * H - 2) as t:
                for g in range(G):
                    row_step(t, 1, g)

            def col_step(u, k):
                for g in range(G):
                    pe.wait_ge(s_k[g], u)
                    for si, s in enumerate(SHIFTS):
                        lo, hi = max(0, -s), min(HP, HP - s)
                        last = mm(banks[CONV[g]][:, lo * BG:hi * BG], hw[:, k, si],
                                  kbuf[:, g, lo + s:hi + s].rearrange("p j b -> p (j b)"),
                                  start=si == 0, stop=si == SH - 1)
                    last.then_inc(s_hm[g], 1)

            with pe.Fori(1, W) as u:
                col_step(u, 0)
            with pe.Fori(W, 2 * W - 2) as u:
                col_step(u, 1)

            def center_tokens(j, c):
                n = CH * j + c
                pe.wait_ge(s_t, n + 1)
                if c > 0:
                    pe.wait_ge(s_ln2, n)
                elif later(j):
                    pe.wait_ge(s_sm, SMN * (j - 1) + 1)
                mm(banks[TLN[c % 2]][:, 0:NC], center_w[:, :],
                   cols[:, j, c * BC:(c + 1) * BC].rearrange("p b w -> p (b w)"),
                   start=True, stop=True).then_inc(s_d2, 1)

            def variance_tokens(j, c):
                n = CH * j + c
                pe.wait_ge(s_sq2, n + 1)
                if later(n):
                    pe.wait_ge(s_xn2, n)
                mm(banks[TLN[1 - c % 2]][:, 0:NC], mean_w[:, :], sq[:, c % 2], start=True, stop=True).then_inc(s_v2, 1)

            def tile_lo(p):
                return min(p * TN, REG - TN)

            def logits(j, slot, c):
                pe.wait_ge(s_tl, 2 * (CH * j + c + 1))
                if c == 0:
                    pe.wait_ge(s_ln2, CH * (j + 1))
                for p in range(TILES):
                    if c * NC < tile_lo(p) + TN <= (c + 1) * NC:
                        for q in range(2):
                            k = 2 * E * (2 * p + q)
                            last = mm(banks[LOG][:, k:k + 2 * E], tok[:, slot, q, tile_lo(p):tile_lo(p) + TN],
                                      rm[:, :, :].rearrange("p l e -> p (l e)"), start=True, stop=True)
                if c == CH - 1:
                    last.then_inc(s_lt, 1)

            def experts(j, slot, p):
                n, span = TILES * j + p, slice(tile_lo(p), tile_lo(p) + TN)
                for q in range(2):
                    sem_g, engine = (s_ga, "act") if q == 1 and (p - 2) % TILES in ACT_TILES else (s_g, "dve")
                    if p >= 2:
                        pe.wait_ge(sem_g, gates(engine, j, p - 2, q))
                    elif later(j):
                        pe.wait_ge(sem_g, gates(engine, j - 1, p - 2 + TILES, q))
                    for b in range(2):
                        last = mm(banks[OUTS[(TILES * slot + p) % 2][q]][:, 0:E * C], tok[:, slot, q, span], em[:, b],
                                  start=b == 0, stop=b == 1)
                    last.then_inc(s_p, 1)

            def sum_experts(j, slot, p):
                n = TILES * j + p
                pe.wait_ge(s_ps, n + 1)
                pe.wait_ge(s_o, n + 1)
                for e in range(E // 2):
                    last = mm(banks[SUM[(TILES * slot + p) % 2]][:, 0:TN], stage(slot, p)[:, e], ident[:, :],
                              start=e == 0, stop=e == E // 2 - 1, is_transpose=True)
                last.then_inc(s_y, 1)

            def region(j, slot, now, ahead):
                for p in range(TILES):
                    if j is not None:
                        experts(j, slot, p)
                    if now is not None:
                        if p in (1, 3):
                            variance_tokens(now, (p + 3) // 2)
                        if p in (0, 2):
                            center_tokens(now, p // 2 + 2)
                        if p in (5, 6):
                            for c in ((0, 1), (2, 3))[p - 5]:
                                logits(now, 1 - slot, c)
                    if ahead is not None:
                        if p == 9:
                            center_tokens(ahead, 0)
                        if p in (10, 12):
                            variance_tokens(ahead, p // 2 - 5)
                        if p == 11:
                            center_tokens(ahead, 1)
                    if j is not None:
                        if p >= LAG:
                            sum_experts(j, slot, p - LAG)
                        elif later(j):
                            sum_experts(j - 1, 1 - slot, TILES + p - LAG)

            pe.wait_ge(s_em, 7)
            region(None, 0, None, 0)
            region(None, 1, 0, 1)
            region(0, 0, 1, 2)
            with pe.Fori(1, HP // 2 - 1) as i:
                region(2 * i - 1, 1, 2 * i, 2 * i + 1)
                region(2 * i, 0, 2 * i + 1, 2 * i + 2)
            region(HP - 3, 1, HP - 2, HP - 1)
            region(HP - 2, 0, HP - 1, None)
            region(HP - 1, 1, None, None)
            for p in range(TILES - LAG, TILES):
                sum_experts(HP - 1, 1, p)


_INS = ['x', 'L0_conv_w_d', 'L0_conv_w_u', 'L0_conv_w_r', 'L0_conv_w_l',
        'L0_ffn_router_w', 'L0_ffn_router_b', 'L0_ffn_expert_w', 'L0_ffn_expert_b']


def kernel(**inputs):
    import numpy as np
    import concourse.bacc as bacc
    from concourse.bass_utils import run_bass_kernel_spmd

    nc = bacc.Bacc("TRN2", target_bir_lowering=False, num_devices=1)
    arrays, args = {}, []
    for name in _INS:
        a = np.ascontiguousarray(inputs[name])
        arrays[name] = a
        args.append(nc.dram_tensor(name, a.shape, mybir.dt.from_np(a.dtype), kind="ExternalInput").ap())
    shape = arrays['x'].shape
    args.append(nc.dram_tensor("result", shape, F32, kind="ExternalOutput").ap())
    metaformer_kernel(nc, *args)
    r = run_bass_kernel_spmd(nc, [arrays], core_ids=[0])
    return r.results[0]["result"]
```

```python
from contextlib import ExitStack

import concourse.bass as bass
from concourse import mybir

F32 = mybir.dt.float32
F32R = mybir.dt.float32r
ALU = mybir.AluOpType
ACT = mybir.ActivationFunctionType
AX = mybir.AxisListType


def metaformer_kernel(nc, x, w_d, w_u, w_r, w_l, router_w, router_b, expert_w, expert_b, out):
    B, C, H, W = x.shape
    TAPS = w_d.shape[-1]
    E = expert_w.shape[0]
    P = 2 * C
    HP, WP = H // 2, W // 2
    SH = TAPS // 2 + 1
    SHIFTS = [0, -1, 1, -2, 2]
    TAPE = TAPS + 1
    G = 2
    BG = B // G
    REG = B * W
    NV, NH = BG * WP, HP * BG
    CH = 4
    BC = B // CH
    NC = REG // CH
    TN = 128
    TILES = -(-REG // TN)
    TAIL = REG - (TILES - 1) * TN
    NG = TILES * 2
    BIG = 1.0e30

    ctx = ExitStack()
    with ctx:
        def sb(name, shape, dt=F32):
            return ctx.enter_context(nc.sbuf_tensor(name, shape, dt))

        def sem(name):
            return ctx.enter_context(nc.semaphore(name))

        act_buf = sb("act_buf", [P, HP * REG])
        rows = act_buf[:, :].rearrange("p (h b w) -> p h b w", h=H, b=B)
        cols = act_buf[:, :].rearrange("p (j b w) -> p j b w", j=HP, b=B)
        x_in = sb("x_in", [P, 2, B, W])
        parts = sb("parts", [P, 2 * 2 * REG], F32R)
        nwv = SH * P
        vw = parts[:, 0:4 * nwv].rearrange("p (k l s m) -> p k l s m", k=2, l=2, s=SH)
        NPAD = BG * (WP + 2)
        carry = parts[:, 4 * nwv:4 * nwv + 2 * G * NPAD].rearrange("p (l g b w) -> p l g b w", l=2, g=G, b=BG)
        tok = parts[:, :].rearrange("p (s q n) -> p s q n", s=2, q=2)
        NSM = NG * E
        scratch = sb("scratch", [P, 2 * E * P + 9 * NSM])
        raw_w = scratch[:, 0:4 * C * TAPS].rearrange("p (k n) -> p k n", k=4)
        tape = act_buf[:, (HP * REG - 4 * C * TAPE):].rearrange("p (k t c) -> p k t c", k=4, t=TAPE)
        new_row = scratch[:, 0:2 * 2 * G * NV].rearrange("p (a q g n) -> p a q g n", a=2, q=2, g=G)
        sm = scratch[:, 2 * E * P:].rearrange("p (k n e) -> p k n e", k=9, e=E)
        logit, hit, first, rest, second, gate1, gate2 = (sm[:, k] for k in range(7))
        gate = [sm[:, 7], sm[:, 8]]
        late = sb("late", [P, SH * 2 * P])
        hw = late[:, 0:2 * nwv].rearrange("p (k s m) -> p k s m", k=2, s=SH)
        more = sb("more", [P, E * P])
        x_parts = sb("x_parts", [P, 2, 2, NC], F32R)
        sq_parts = parts[:, 2 * 2 * REG - 2 * 2 * NC:].rearrange("p (b l n) -> p b l n", b=2, l=2)
        gated = [scratch[:, 0:E * P], scratch[:, E * P:2 * E * P], late[:, 0:E * P], more[:, :]]
        gated = [g.rearrange("p (e m) -> p e m", e=E) for g in gated]
        early = act_buf[:, (HP - 8) * REG:(HP - 8) * REG + 3 * 4 * NC].rearrange("p (k b n) -> p k b n", k=3, b=4)
        kbuf = sb("kbuf", [P, G, HP, BG])
        sq = sb("sq", [P, 2, NC])
        lnv = sb("lnv", [P, 2, NC])
        rstd = sb("rstd", [P, 2, NC])
        xn = sb("xn", [P, NC])
        ident = sb("ident", [P, P])
        mean_w = sb("mean_w", [P, P])
        center_w = sb("center_w", [P, P])
        mean_r = sb("mean_r", [P, P], F32R)
        center_r = sb("center_r", [P, P], F32R)
        eps_c = sb("eps_c", [P, 3])
        rank_w = sb("rank_w", [P, NG, E])
        ew = sb("ew", [P, E * C + E])
        eb = sb("eb", [P, E * C + E])
        em = sb("em", [P, 2, E * C], F32R)
        rm = sb("rm", [P, 2, E], F32R)
        best = sb("best", [P, 6, NG])

        banks = [ctx.enter_context(nc.psum_tensor(f"bank{i}", [P, 512], F32)) for i in range(8)]

        CONV = [0, 1]
        CEN, VAR = [2, 3], [4, 5]
        OUTS = [[0, 1], [2, 3]]
        TLN = [4, 5]
        LOG = TLN[0]
        SUM = [6, 7]
        ACT_TILES = (5, 6, 7, 8, 9, 10)
        LAG = 2
        SEQ = 2 * TILES

        def gates(engine, j, p, q):
            mine = [(a, b) for a in range(TILES) for b in range(2) if (a in ACT_TILES and b == 1) == (engine == "act")]
            return len(mine) * j + sum(m <= (p, q) for m in mine)

        def stage_of(k):
            k = k % SEQ
            return k % 4 if k < SEQ - 6 else (k - (SEQ - 6)) % 3

        def stage(slot, p):
            return gated[stage_of(TILES * slot + p)]

        def stage_age(slot, p):
            k = TILES * slot + p
            return next(d for d in range(1, SEQ) if stage_of(k - d) == stage_of(k))

        def later(n):
            return not isinstance(n, int) or n > 0

        SMN = 18
        GAP_STEP = 12
        STEP_AT = [(7, 1), (7, 2), (8, 0), (8, 1), (8, 2), (9, 0), (9, 1), (9, 2), (10, 0), (10, 1), (10, 2),
                   (10, 2), (11, 0), (11, 1), (11, 1), (11, 2), (12, 0), (12, 1)]
        LOGITS_AT = (4, 5, 5, 6)
        EXP_TILE = STEP_AT[GAP_STEP - 1][0] + 1

        s_wraw_v = sem("s_wraw_v")
        s_wraw_h = sem("s_wraw_h")
        s_eraw = sem("s_eraw")
        s_x = [sem("s_x0"), sem("s_x1")]
        s_id0 = sem("s_id0")
        s_id = sem("s_id")
        s_cst = sem("s_cst")
        s_tape0 = sem("s_tape0")
        s_tape = sem("s_tape")
        s_wt = sem("s_wt")
        s_wh = sem("s_wh")
        s_wv = sem("s_wv")
        s_cmean = sem("s_cmean")
        s_em = sem("s_em")
        s_cr = sem("s_cr")
        s_xp = sem("s_xp")
        s_sqa = sem("s_sqa")
        s_sqb = sem("s_sqb")
        s_d = sem("s_d")
        s_sq = sem("s_sq")
        s_v = sem("s_v")
        s_ln = sem("s_ln")
        s_r = sem("s_r")
        s_xn = sem("s_xn")
        s_h = [sem(f"s_h{g}") for g in range(G)]
        s_l = [sem(f"s_l{g}") for g in range(G)]
        s_mm = [sem(f"s_mm{g}") for g in range(G)]
        s_new = [sem(f"s_new{g}") for g in range(G)]
        s_trv = sem("s_trv")
        s_tra = sem("s_tra")
        s_k = [sem(f"s_k{g}") for g in range(G)]
        s_hm = [sem(f"s_hm{g}") for g in range(G)]
        s_cb = [sem(f"s_cb{g}") for g in range(G)]
        s_t = sem("s_t")
        s_d2 = sem("s_d2")
        s_sq2 = sem("s_sq2")
        s_v2 = sem("s_v2")
        s_ln2 = sem("s_ln2")
        s_r2 = sem("s_r2")
        s_xn2 = sem("s_xn2")
        s_th = sem("s_th")
        s_tl = sem("s_tl")
        s_lt = sem("s_lt")
        s_sm = sem("s_sm")
        s_g1 = sem("s_g1")
        s_ex = sem("s_ex")
        s_p = sem("s_p")
        s_g = sem("s_g")
        s_ga = sem("s_ga")
        s_ps = sem("s_ps")
        s_y = sem("s_y")
        s_o = sem("s_o")
        s_out = sem("s_out")

        block = ctx.enter_context(nc.Block())

        def pair_view(dram, j, q):
            return dram.rearrange("b c (j q) w -> q j c b w", q=2)[q, j]

        def load_conv(engine, k, w):
            loaded = s_wraw_v if k < 2 else s_wraw_h
            for q in range(2):
                engine.dma_start(raw_w[q * C:(q + 1) * C, k], w.rearrange("o i a b -> o (i a b)")).then_inc(loaded, 16)

        @block.sync
        def _(sp):
            def load(j, slot):
                for q in range(2):
                    sp.dma_start(x_in[q * C:(q + 1) * C, slot], pair_view(x, j, q)).then_inc(s_x[slot], 16)

            load(0, 0)
            load(1, 1)
            load_conv(sp, 2, w_r)
            load_conv(sp, 3, w_l)
            for q in range(2):
                half = slice(q * C, (q + 1) * C)
                sp.dma_start(ew[half, 0:E * C].rearrange("p (e c) -> p e c", e=E),
                             expert_w.rearrange("e d c -> d e c")).then_inc(s_eraw, 16)
                sp.dma_start(ew[half, E * C:], router_w).then_inc(s_eraw, 16)
            sp.dma_start(eb[:, 0:E * C],
                         expert_b.rearrange("(o e) c -> o (e c)", o=1).broadcast_to([P, E * C])).then_inc(s_eraw, 16)
            sp.dma_start(eb[:, E * C:], router_b.rearrange("(o e) -> o e", o=1).broadcast_to([P, E])).then_inc(s_eraw, 16)
            with sp.Fori(1, HP // 2) as i:
                for slot in range(2):
                    sp.wait_ge(s_d, 2 * CH * i - CH + CH * slot)
                    load(2 * i + slot, slot)
            for slot in range(2):
                sp.wait_ge(s_d, CH * (HP - 1 + slot))
                load(slot, slot)

            def store(j):
                sp.wait_ge(s_o, 2 + TILES * (j + 1))
                for q in range(2):
                    sp.dma_start(pair_view(out, j, q), cols[q * C:(q + 1) * C, j]).then_inc(s_out, 16)

            def reload(j, slot):
                sp.wait_ge(s_t, CH * (j - 1))
                load(j, slot)

            reload(2, 0)
            with sp.Fori(0, HP // 2 - 2) as i:
                for slot in range(2):
                    reload(2 * i + slot + 3, 1 - slot)
                    store(2 * i + slot)
            reload(HP - 1, 1)
            for j in range(HP - 4, HP):
                store(j)
            sp.wait_ge(s_out, HP * 32)

        @block.gpsimd
        def _(pool):
            nc.gpsimd.memset(ident[:, :], 0.0).then_inc(s_id0, 1)
            pool.wait_ge(s_id0, 1)
            nc.gpsimd.affine_select(out=ident[:, :], in_=ident[:, :], compare_op=ALU.not_equal, fill=1.0,
                                    base=0, pattern=[[-1, P]], channel_multiplier=1).then_inc(s_id, 1)

            zero = eps_c[:, 2:3]

            def split_x(slot, c, n, b):
                m = n - 2 * CH
                src = x_in[:, slot, c * BC:(c + 1) * BC].rearrange("p b w -> p (b w)")
                pool.wait_ge(s_d, n - 1)
                nc.gpsimd.tensor_tensor(x_parts[:, b, 0], src, zero.to_broadcast([P, NC]), ALU.add).then_inc(s_xp, 1)
                pool.wait_ge(s_xp, 2 * m + 1)
                nc.gpsimd.tensor_tensor(x_parts[:, b, 1], src, x_parts[:, b, 0].bitcast(F32), ALU.subtract).then_inc(s_xp, 1)

            with pool.Fori(1, HP // 2) as i:
                for slot in range(2):
                    pool.wait_ge(s_x[slot], 32 * (i + 1))
                    for c in range(CH):
                        split_x(slot, c, CH * (2 * i + slot) + c, c % 2)

            def residual(j, slot, c):
                t = cols[:, j, c * BC:(c + 1) * BC]
                nc.gpsimd.tensor_tensor(t, t, x_in[:, slot, c * BC:(c + 1) * BC], ALU.add).then_inc(s_t, 1)

            def pair_sums(j, slot, p):
                pool.wait_ge(s_g, gates("dve", j, p, 1))
                if p in ACT_TILES:
                    pool.wait_ge(s_ga, gates("act", j, p, 1))
                buf = stage(slot, p)
                nc.gpsimd.tensor_tensor(buf[:, 0:4], buf[:, 0:4], buf[:, 4:8], ALU.add).then_inc(s_ps, 1)

            def region(j, slot, now, ahead, visit):
                for p in range(TILES):
                    if now is not None and p == TILES - 1:
                        pool.wait_ge(s_sm, SMN * now + SMN - 3)
                        nc.gpsimd.tensor_tensor(gate1, first, best[:, 0].unsqueeze(2).to_broadcast([P, NG, E]),
                                                ALU.mult).then_inc(s_g1, 1)
                    if ahead is not None and p in (6, 8, 10, 12):
                        if p == 6:
                            pool.wait_ge(s_x[slot], 32 * (HP // 2 + visit))
                        residual(ahead, slot, p // 2 - 3)
                    if j is not None:
                        pair_sums(j, slot, p)

            for g in range(G):
                pool.wait_ge(s_cb[g], 2 * W - 2)
            region(None, 0, None, 0, 1)
            region(None, 1, 0, 1, 1)
            region(0, 0, 1, 2, 2)
            with pool.Fori(1, HP // 2 - 1) as i:
                region(2 * i - 1, 1, 2 * i, 2 * i + 1, i + 1)
                region(2 * i, 0, 2 * i + 1, 2 * i + 2, i + 2)
            region(HP - 3, 1, HP - 2, HP - 1, HP // 2)
            region(HP - 2, 0, HP - 1, None, None)
            region(HP - 1, 1, None, None, None)

        NCST = 4 + E + 3 + 1

        @block.scalar
        def _(act):
            load_conv(act, 0, w_d)
            load_conv(act, 1, w_u)
            nc.scalar.preload_act_table_set("natural_log_exp_and_others")
            def square(n, b):
                act.wait_ge(s_d, n + 1)
                for dst in (sq_parts[:, b, 0], sq[:, b]):
                    act.activation(dst, banks[CEN[b]][:, 0:NC], ACT.Square).then_inc(s_sqa, 1)

            def inv_std(n, b):
                act.wait_ge(s_v, n + 1)
                act.wait_ge(s_xn, n + 1)
                act.activation(lnv[:, b], banks[VAR[b]][:, 0:NC], ACT.Ln, bias=eps_c[:, 0:1]).then_inc(s_ln, 1)
                act.wait_ge(s_ln, n + 1)
                act.activation(rstd[:, b], lnv[:, b], ACT.Exp, scale=-0.5).then_inc(s_r, 1)

            act.wait_ge(s_cst, NCST)
            for k in range(2 * CH + 2):
                if k < 2 * CH:
                    act.wait_ge(s_d, k + 1)
                    act.activation(early[:, 0, k % 4], banks[k % 4][:, 0:NC], ACT.Square).then_inc(s_sq, 1)
                if k >= 2:
                    act.wait_ge(s_v, k - 1)
                    if k >= 6:
                        act.wait_ge(s_xn, k - 3)
                    act.activation(early[:, 1, (k - 2) % 4], banks[4 + (k - 2) % 4][:, 0:NC], ACT.Ln,
                                   bias=eps_c[:, 0:1]).then_inc(s_ln, 1)
                    act.wait_ge(s_ln, k - 1)
                    act.activation(early[:, 2, (k - 2) % 4], early[:, 1, (k - 2) % 4], ACT.Exp,
                                   scale=-0.5).then_inc(s_r, 1)
            for n in range(8):
                k = n // 2
                act.wait_ge(s_wt, n + 1)
                lo, hi = (0, 4) if n % 2 == 0 else (4, SH)
                dst = vw[:, k, 0, lo:hi] if k < 2 else hw[:, k - 2, lo:hi]
                act.activation(dst, banks[n][:, 0:(hi - lo) * P].rearrange("p (s m) -> p s m", m=P),
                               ACT.Copy).then_inc(s_wh, 1)

            act.wait_ge(s_xn, 2 + 2 * CH)
            for g in range(G):
                act.activation(carry[:, 0, g, :, 1:WP + 1],
                               rows[:, 0, g * BG:(g + 1) * BG], ACT.Copy).then_inc(s_h[g], 1)

            def down_round(t, g):
                act.wait_ge(s_new[g], t)
                act.activation(carry[:, 0, g, :, 1:WP + 1],
                               rows[:, t, g * BG:(g + 1) * BG], ACT.Copy).then_inc(s_h[g], 1)

            def down_pair(i, norm):
                for m in range(CH):
                    if norm:
                        square(CH * (i + 2) + m, m % 2)
                    down_round(2 * i + 1 + m // G, m % G)
                    if norm:
                        inv_std(CH * (i + 2) + m, m % 2)

            with act.Fori(0, (HP - 2) // 2) as i:
                for u in range(2):
                    down_pair(2 * i + u, True)
            down_pair(HP - 2, False)
            for g in range(G):
                down_round(H - 1, g)

            def round_row(t, par, q):
                for g in range(G):
                    act.wait_ge(s_new[g], t)
                    act.activation(carry[:, 0, g, :, 1:WP + 1],
                                   new_row[:, par, q, g].rearrange("p (b w) -> p b w", b=BG), ACT.Copy).then_inc(s_h[g], 1)

            def move_cross(j, par):
                for g in range(G):
                    for q in range(2):
                        dst = cols[q * C:(q + 1) * C, j, g * BG:(g + 1) * BG].rearrange("p b (w a) -> p b w a", a=2)[:, :, :, 1 - q]
                        src = new_row[(1 - q) * C:(2 - q) * C, par, q, g].rearrange("p (b w) -> p b w", b=BG)
                        act.activation(dst, src, ACT.Copy).then_inc(s_tra, 1)

            round_row(H, 1, 0)
            act.wait_ge(s_trv, G)
            move_cross(HP - 1, 1)
            with act.Fori(0, (HP - 2) // 2) as i:
                for par in range(2):
                    t = 4 * i + 2 * par + H + 1
                    round_row(t, par, 1)
                    round_row(t + 1, par, 0)
                    move_cross(HP - 2 - par - 2 * i, par)
            round_row(2 * H - 3, 0, 1)
            for g in range(G):
                act.wait_ge(s_new[g], 2 * H - 2)
            move_cross(0, 0)

            def copy_back(u, w):
                for g in range(G):
                    act.wait_ge(s_k[g], u + 1)
                    act.activation(cols[:, :, g * BG:(g + 1) * BG, w], kbuf[:, g], ACT.Copy).then_inc(s_cb[g], 1)

            with act.Fori(1, W) as u:
                copy_back(u, u)
            with act.Fori(W, 2 * W - 2) as u:
                w = u * -1 + (2 * W - 2)
                copy_back(u, w)

            def norm_square(j, c, bank=None):
                act.wait_ge(s_d2, CH * j + c + 1)
                src = banks[TLN[c % 2] if bank is None else bank]
                act.activation(sq[:, c % 2], src[:, 0:NC], ACT.Square).then_inc(s_sq2, 1)

            def norm_std(j, c, bank=None):
                n = CH * j + c
                src = banks[TLN[1 - c % 2] if bank is None else bank]
                act.wait_ge(s_v2, n + 1)
                act.activation(lnv[:, c % 2], src[:, 0:NC], ACT.Ln, bias=eps_c[:, 1:2]).then_inc(s_ln2, 1)
                act.wait_ge(s_ln2, n + 1)
                act.activation(rstd[:, c % 2], lnv[:, c % 2], ACT.Exp, scale=-0.5).then_inc(s_r2, 1)

            def first_part(j, slot, c):
                act.wait_ge(s_xn2, CH * j + c + 1)
                if c == 0 and later(j - 1):
                    act.wait_ge(s_p, 2 * TILES * (j - 1))
                for q in range(2):
                    half = slice(q * C, (q + 1) * C)
                    act.activation(tok[half, slot, q, c * NC:(c + 1) * NC], xn[half, :], ACT.Identity,
                                   bias=1.0).then_inc(s_th, 1)

            def exponential(j):
                act.wait_ge(s_sm, SMN * j + GAP_STEP)
                act.activation(best[:, 3], best[:, 2], ACT.Exp).then_inc(s_ex, 1)

            def gate_odd(j, slot, p):
                n = TILES * j + p
                act.wait_ge(s_sm, SMN * (j + 1))
                if later(n - stage_age(slot, p) + 1):
                    act.wait_ge(s_y, n - stage_age(slot, p) + 1)
                act.wait_ge(s_p, 2 * n + 2)
                for e in range(E):
                    last = act.activation(stage(slot, p)[:, e, C:P], banks[OUTS[(TILES * slot + p) % 2][1]][:, e * C:(e + 1) * C],
                                          ACT.Copy, scale=gate[slot][:, 2 * p + 1, e:e + 1])
                last.then_inc(s_ga, 1)

            def region(j, slot, now, ahead):
                for p in range(TILES):
                    if now is not None and p == EXP_TILE:
                        exponential(now)
                    if now is not None and j is not None:
                        if p in (0, 2, 4):
                            first_part(now, 1 - slot, p // 2 + 1)
                        if p in (0, 2):
                            norm_square(now, p // 2 + 2)
                        if p in (1, 3):
                            norm_std(now, (p + 3) // 2)
                    if ahead is not None:
                        if p == 9:
                            norm_square(ahead, 0)
                        if p == 10:
                            norm_std(ahead, 0)
                        if p == 11:
                            first_part(ahead, slot, 0)
                            norm_square(ahead, 1)
                        if p == 12:
                            norm_std(ahead, 1)
                    if j is not None and p in ACT_TILES:
                        gate_odd(j, slot, p)

            norm_square(0, 0, 0)
            for c in range(CH):
                if c < CH - 1:
                    norm_square(0, c + 1, c + 1)
                if c >= 2:
                    act.wait_ge(s_xn2, c - 1)
                norm_std(0, c, TLN[0] + c)
                first_part(0, 0, c)
            region(None, 1, 0, 1)
            region(0, 0, 1, 2)
            with act.Fori(1, HP // 2 - 1) as i:
                region(2 * i - 1, 1, 2 * i, 2 * i + 1)
                region(2 * i, 0, 2 * i + 1, 2 * i + 2)
            region(HP - 3, 1, HP - 2, HP - 1)
            region(HP - 2, 0, HP - 1, None)
            region(HP - 1, 1, None, None)

        @block.vector
        def _(dve):
            nc.vector.memset(best[:, :, :], 0.0).then_inc(s_xn, 2)
            for edge in (0, WP + 1):
                for k in range(2):
                    nc.vector.memset(carry[:, k, :, :, edge].bitcast(F32), 0.0).then_inc(s_tape0, 1)
            for q in range(2):
                nc.vector.memset(tape[q * C:(q + 1) * C, :, (1 - q) * TAPS], 0.0).then_inc(s_tape0, 1)
            nc.vector.memset(lnv[:, 0, 0:1], 0.0).then_inc(s_o, 2)
            nc.vector.memset(lnv[:, 0, 1:2], 0.0).then_inc(s_tra, 1)
            for g in range(G):
                nc.vector.memset(lnv[:, 1, g:g + 1], 0.0).then_inc(s_cb[g], 1)
            for q in range(2):
                for a in range(2):
                    nc.vector.memset(mean_w[q * C:(q + 1) * C, a * C:(a + 1) * C],
                                     1.0 / C if a == q else 0.0).then_inc(s_cst, 1)
            for e in range(E):
                nc.vector.memset(rank_w[:, :, e], float(E - e)).then_inc(s_cst, 1)
            nc.vector.memset(eps_c[:, 0:1], 1.0e-6).then_inc(s_cst, 1)
            nc.vector.memset(eps_c[:, 1:2], 1.0e-5).then_inc(s_cst, 1)
            nc.vector.memset(eps_c[:, 2:3], 0.0).then_inc(s_cst, 1)
            dve.wait_ge(s_id, 1)
            dve.wait_ge(s_cst, 4)
            nc.vector.tensor_tensor(center_w[:, :], ident[:, :], mean_w[:, :], ALU.subtract).then_inc(s_cst, 1)
            dve.wait_ge(s_wraw_v, 4 * 16)
            dve.wait_ge(s_tape0, 6)
            def space_taps(k):
                for q in range(2):
                    nc.vector.tensor_copy(tape[q * C:(q + 1) * C, k, q:q + TAPS],
                                          raw_w[q * C:(q + 1) * C, k].rearrange("p (c t) -> p t c", t=TAPS)).then_inc(s_tape, 1)

            space_taps(0)
            space_taps(1)
            dve.wait_ge(s_cst, NCST)
            nc.vector.tensor_copy(mean_r[:, :], mean_w[:, :]).then_inc(s_cr, 1)
            nc.vector.tensor_copy(center_r[:, :], center_w[:, :]).then_inc(s_cr, 1)

            def normalise_rows(n, b, j, c, centred=None, inv=None):
                if centred is None:
                    centred, inv = banks[CEN[b]][:, 0:NC], rstd[:, b]
                dve.wait_ge(s_r, n + 1)
                for q in range(2):
                    for a in range(2):
                        half = slice(q * C, (q + 1) * C)
                        src = centred[half].rearrange("p (b w a) -> p b w a", b=BC, a=2)[:, :, :, a]
                        scl = inv[half].rearrange("p (b w a) -> p b w a", b=BC, a=2)[:, :, :, a]
                        last = nc.vector.tensor_tensor(rows[a * C:(a + 1) * C, 2 * j + q, c * BC:(c + 1) * BC],
                                                       src, scl, ALU.mult)
                last.then_inc(s_xn, 1)

            for k in range(2 * CH):
                normalise_rows(k, k % 4, k // CH, k % CH, banks[k % 4][:, 0:NC], early[:, 2, k % 4])

            dve.wait_ge(s_wraw_h, 4 * 16)
            space_taps(2)
            space_taps(3)
            for n in range(4):
                lo, hi = (0, 4) if n % 2 == 0 else (4, SH)
                dve.wait_ge(s_wh, n + 1)
                nc.vector.tensor_tensor(vw[:, n // 2, 1, lo:hi], banks[n][:, 0:(hi - lo) * P].rearrange("p (s m) -> p s m", m=P),
                                        vw[:, n // 2, 0, lo:hi].bitcast(F32), ALU.subtract).then_inc(s_wv, 1)

            for g in range(G):
                dve.wait_ge(s_h[g], 1)
                nc.vector.tensor_tensor(carry[:, 1, g, :, 1:WP + 1], rows[:, 0, g * BG:(g + 1) * BG],
                                        carry[:, 0, g, :, 1:WP + 1].bitcast(F32),
                                        ALU.subtract).then_inc(s_l[g], 1)

            dve.wait_ge(s_cmean, 1)
            dve.wait_ge(s_eraw, 6 * 16)
            nc.vector.tensor_tensor(ew[:, 0:E * C], ew[:, 0:E * C], banks[SUM[0]][:, 0:E * C], ALU.subtract).then_inc(s_em, 1)
            nc.vector.tensor_tensor(ew[:, E * C:], ew[:, E * C:], banks[SUM[1]][:, 0:E], ALU.subtract).then_inc(s_em, 1)
            dve.wait_ge(s_em, 2)
            nc.vector.scalar_tensor_tensor(ew[:, :], eb[:, :], 1.0 / C, ew[:, :], ALU.mult, ALU.add).then_inc(s_em, 1)
            dve.wait_ge(s_em, 3)
            nc.vector.tensor_copy(em[:, 0], ew[:, 0:E * C]).then_inc(s_em, 1)
            nc.vector.tensor_copy(rm[:, 0], ew[:, E * C:]).then_inc(s_em, 1)
            dve.wait_ge(s_em, 5)
            nc.vector.tensor_tensor(em[:, 1], ew[:, 0:E * C], em[:, 0].bitcast(F32), ALU.subtract).then_inc(s_em, 1)
            nc.vector.tensor_tensor(rm[:, 1], ew[:, E * C:], rm[:, 0].bitcast(F32), ALU.subtract).then_inc(s_em, 1)

            def down_step(t, g, between):
                row = rows[:, t, g * BG:(g + 1) * BG]
                conv = banks[CONV[g]][:, 0:NV].rearrange("p (b w) -> p b w", b=BG)
                dve.wait_ge(s_mm[g], t)
                nc.vector.scalar_tensor_tensor(row, conv, 0.0, row, ALU.max, ALU.add).then_inc(s_new[g], 1)
                between()
                dve.wait_ge(s_h[g], t + 1)
                nc.vector.tensor_tensor(carry[:, 1, g, :, 1:WP + 1], row,
                                        carry[:, 0, g, :, 1:WP + 1].bitcast(F32), ALU.subtract).then_inc(s_l[g], 1)

            def down_pair(i, before, norm):
                for m in range(CH):
                    def between():
                        if norm:
                            n = CH * i + m + 1
                            dve.wait_ge(s_sqa, 2 * n)
                            nc.vector.tensor_tensor(sq_parts[:, m % 2, 1], sq[:, m % 2],
                                                    sq_parts[:, m % 2, 0].bitcast(F32), ALU.subtract).then_inc(s_sqb, 1)
                        if m == 0 and before:
                            normalise_rows(CH * (i + 1) + CH - 1, 1, i + 1, CH - 1)
                        if m > 0 and norm:
                            normalise_rows(CH * (i + 2) + m - 1, (m - 1) % 2, i + 2, m - 1)
                    down_step(2 * i + 1 + m // G, m % G, between)

            down_pair(0, False, True)
            down_pair(1, True, True)
            with dve.Fori(1, (HP - 2) // 2) as i:
                for u in range(2):
                    down_pair(2 * i + u, True, True)
            down_pair(HP - 2, True, False)
            for g in range(G):
                down_step(H - 1, g, lambda: None)

            def up_step(t, h, par, q):
                for g in range(G):
                    row = rows[:, h, g * BG:(g + 1) * BG].rearrange("p b w -> p (b w)")
                    dve.wait_ge(s_mm[g], t)
                    nc.vector.scalar_tensor_tensor(new_row[:, par, q, g], banks[CONV[g]][:, 0:NV], 0.0, row,
                                                   ALU.max, ALU.add).then_inc(s_new[g], 1)
                    dve.wait_ge(s_h[g], t + 1)
                    nc.vector.tensor_tensor(carry[:, 1, g, :, 1:WP + 1],
                                            new_row[:, par, q, g].rearrange("p (b w) -> p b w", b=BG),
                                            carry[:, 0, g, :, 1:WP + 1].bitcast(F32), ALU.subtract).then_inc(s_l[g], 1)

            def move_same(j, par):
                for g in range(G):
                    for q in range(2):
                        half = slice(q * C, (q + 1) * C)
                        dst = cols[half, j, g * BG:(g + 1) * BG].rearrange("p b (w a) -> p b w a", a=2)[:, :, :, q]
                        src = new_row[half, par, q, g].rearrange("p (b w) -> p b w", b=BG)
                        nc.vector.tensor_copy(dst, src).then_inc(s_trv, 1)

            PM = 2 * G
            for g in range(G):
                nc.vector.tensor_copy(new_row[:, 1, 1, g].rearrange("p (b w) -> p b w", b=BG),
                                      rows[:, H - 1, g * BG:(g + 1) * BG]).then_inc(s_trv, 1)
            up_step(H, H - 2, 1, 0)
            dve.wait_ge(s_trv, G)
            move_same(HP - 1, 1)
            with dve.Fori(0, (HP - 2) // 2) as i:
                h_odd = [i * -4 + (H - 3 - 2 * par) for par in range(2)]
                h_even = [i * -4 + (H - 4 - 2 * par) for par in range(2)]
                for par in range(2):
                    t = 4 * i + 2 * par + H + 1
                    if par == 1:
                        dve.wait_ge(s_tra, PM * (2 * i + 1) + 1)
                    else:
                        dve.wait_ge(s_tra, PM * 2 * i + 1)
                    up_step(t, h_odd[par], par, 1)
                    up_step(t + 1, h_even[par], par, 0)
                    move_same(HP - 2 - par - 2 * i, par)
            dve.wait_ge(s_tra, PM * (HP - 2) + 1)
            up_step(2 * H - 3, 1, 0, 1)
            for g in range(G):
                nc.vector.tensor_copy(new_row[:, 0, 0, g].rearrange("p (b w) -> p b w", b=BG),
                                      rows[:, 0, g * BG:(g + 1) * BG]).then_inc(s_new[g], 1)
            for g in range(G):
                dve.wait_ge(s_new[g], 2 * H - 2)
            move_same(0, 0)

            dve.wait_ge(s_tra, PM * HP + 1)
            dve.wait_ge(s_trv, G + PM * HP)
            for g in range(G):
                nc.vector.tensor_copy(kbuf[:, g], cols[:, :, g * BG:(g + 1) * BG, 0]).then_inc(s_k[g], 1)

            def col_step(u, w):
                for g in range(G):
                    dve.wait_ge(s_hm[g], u)
                    dve.wait_ge(s_cb[g], u)
                    nc.vector.scalar_tensor_tensor(kbuf[:, g], banks[CONV[g]][:, 0:NH].rearrange("p (j b) -> p j b", j=HP), 0.0,
                                                   cols[:, :, g * BG:(g + 1) * BG, w], ALU.max, ALU.add).then_inc(s_k[g], 1)

            with dve.Fori(1, W) as u:
                col_step(u, u)
            with dve.Fori(W, 2 * W - 2) as u:
                w = u * -1 + (2 * W - 2)
                col_step(u, w)

            def flat(j):
                return cols[:, j].rearrange("p b w -> p (b w)")

            def normalise(j, c, bank=None):
                n = CH * j + c
                src = banks[TLN[c % 2] if bank is None else bank]
                dve.wait_ge(s_r2, n + 1)
                if later(n):
                    dve.wait_ge(s_tl, 2 * n)
                nc.vector.tensor_tensor(xn[:, :], src[:, 0:NC], rstd[:, c % 2], ALU.mult).then_inc(s_xn2, 1)

            def second_part(j, slot, c):
                dve.wait_ge(s_th, 2 * (CH * j + c + 1))
                span = slice(c * NC, (c + 1) * NC)
                for q in range(2):
                    half, other = slice(q * C, (q + 1) * C), slice((1 - q) * C, (2 - q) * C)
                    nc.vector.scalar_tensor_tensor(tok[other, slot, q, span], xn[half, :], 1.0,
                                                   tok[half, slot, q, span].bitcast(F32),
                                                   ALU.add, ALU.subtract).then_inc(s_tl, 1)

            def spread(v):
                return v.unsqueeze(2).to_broadcast([P, NG, E])

            m1, m2, gap, ex, den, idx = (best[:, k] for k in range(6))

            def softmax_steps(j, slot):
                v = nc.vector
                return [
                    lambda: v.tensor_reduce(logit, banks[LOG][:, 0:2 * NSM].rearrange("p (n l e) -> p n e l", l=2, e=E), AX.X, ALU.add),
                    lambda: v.tensor_reduce(m1, logit, AX.X, ALU.max),
                    lambda: v.tensor_tensor(hit, logit, spread(m1), ALU.is_equal),
                    lambda: v.tensor_tensor(hit, hit, rank_w[:, :, :], ALU.mult),
                    lambda: v.tensor_reduce(idx, hit, AX.X, ALU.max),
                    lambda: v.tensor_tensor(first, rank_w[:, :, :], spread(idx), ALU.is_equal),
                    lambda: v.scalar_tensor_tensor(rest, first, -BIG, logit, ALU.mult, ALU.add),
                    lambda: v.tensor_reduce(m2, rest, AX.X, ALU.max),
                    lambda: v.tensor_tensor(hit, rest, spread(m2), ALU.is_equal),
                    lambda: v.tensor_tensor(hit, hit, rank_w[:, :, :], ALU.mult),
                    lambda: v.tensor_reduce(idx, hit, AX.X, ALU.max),
                    lambda: v.tensor_tensor(gap, m2, m1, ALU.subtract),
                    lambda: v.tensor_tensor(second, rank_w[:, :, :], spread(idx), ALU.is_equal),
                    lambda: v.tensor_scalar(den, ex, 1.0, None, ALU.add),
                    lambda: v.reciprocal(m1, den),
                    lambda: v.tensor_tensor(m2, ex, m1, ALU.mult),
                    lambda: v.tensor_tensor(gate2, second, spread(m2), ALU.mult),
                    lambda: v.tensor_tensor(gate[slot], gate1, gate2, ALU.add),
                ]

            def softmax(j, slot, at):
                steps = softmax_steps(j, slot)
                for k in range(SMN):
                    if STEP_AT[k] == at:
                        if k == 0:
                            dve.wait_ge(s_lt, j + 1)
                        elif k == GAP_STEP + 1:
                            dve.wait_ge(s_ex, j + 1)
                        elif k == SMN - 1:
                            dve.wait_ge(s_g1, j + 1)
                        if k > 0:
                            dve.wait_ge(s_sm, SMN * j + k)
                        steps[k]().then_inc(s_sm, 1)

            def gate_half(j, slot, p, q):
                n = TILES * j + p
                if q == 0:
                    if p == 0:
                        dve.wait_ge(s_sm, SMN * (j + 1))
                    if later(n - stage_age(slot, p) + 1):
                        dve.wait_ge(s_y, n - stage_age(slot, p) + 1)
                dve.wait_ge(s_p, 2 * n + q + 1)
                src = banks[OUTS[(TILES * slot + p) % 2][q]][:, 0:E * C].rearrange("p (e c) -> p e c", e=E)
                scl = gate[slot][:, 2 * p + q].unsqueeze(2).to_broadcast([P, E, C])
                nc.vector.tensor_tensor(stage(slot, p)[:, :, q * C:(q + 1) * C], src, scl, ALU.mult).then_inc(s_g, 1)

            def add_out(j, slot, p):
                n, par = TILES * j + p, (TILES * slot + p) % 2
                width, off = (TN, 0) if p < TILES - 1 else (TAIL, TN - TAIL)
                dst = flat(j)[:, p * TN:p * TN + width]
                dve.wait_ge(s_y, n + 1)
                nc.vector.tensor_tensor(dst, banks[SUM[par]][:, off:off + width], dst, ALU.add).then_inc(s_o, 1)

            def add_behind(j, slot, p):
                if p >= LAG:
                    add_out(j, slot, p - LAG)
                elif later(j):
                    add_out(j - 1, 1 - slot, TILES + p - LAG)

            def region(j, slot, now, ahead):
                for p in range(TILES):
                    if now is not None and j is not None and p in (0, 2, 4):
                        normalise(now, p // 2 + 1)
                    if ahead is not None and p == 11:
                        normalise(ahead, 0)
                    for part in range(3):
                        if j is not None:
                            if part == 2:
                                add_behind(j, slot, p)
                            elif part == 0 or p not in ACT_TILES:
                                gate_half(j, slot, p, part)
                        if now is not None:
                            softmax(now, 1 - slot, (p, part))
                    if now is not None and j is not None and p in (0, 2, 4):
                        second_part(now, 1 - slot, p // 2 + 1)
                    if ahead is not None and p == 11:
                        second_part(ahead, slot, 0)

            for c in range(CH):
                normalise(0, c, c)
                second_part(0, 0, c)
            region(None, 1, 0, 1)
            region(0, 0, 1, 2)
            with dve.Fori(1, HP // 2 - 1) as i:
                region(2 * i - 1, 1, 2 * i, 2 * i + 1)
                region(2 * i, 0, 2 * i + 1, 2 * i + 2)
            region(HP - 3, 1, HP - 2, HP - 1)
            region(HP - 2, 0, HP - 1, None)
            region(HP - 1, 1, None, None)
            for p in range(TILES - LAG, TILES):
                add_out(HP - 1, 1, p)

        @block.tensor
        def _(pe):
            mm = nc.tensor.matmul

            def center(n, b):
                pe.wait_ge(s_xn, n + 1)
                pe.wait_ge(s_xp, 2 * (n - 2 * CH + 1))
                for l in range(2):
                    last = mm(banks[CEN[b]][:, 0:NC], center_r[:, :], x_parts[:, b, l], start=l == 0, stop=l == 1)
                last.then_inc(s_d, 1)

            def variance(n, b):
                pe.wait_ge(s_sqb, n - 2 * CH + 1)
                for l in range(2):
                    last = mm(banks[VAR[b]][:, 0:NC], mean_r[:, :], sq_parts[:, b, l], start=l == 0, stop=l == 1)
                last.then_inc(s_v, 1)

            pe.wait_ge(s_id, 1)
            pe.wait_ge(s_cst, NCST)
            for k in range(2 * CH + 1):
                if k < 2 * CH:
                    if k % CH == 0:
                        pe.wait_ge(s_x[k // CH], 32)
                    if k >= 4:
                        pe.wait_ge(s_xn, k - 1)
                    c = k % CH
                    mm(banks[k % 4][:, 0:NC], center_w[:, :],
                       x_in[:, k // CH, c * BC:(c + 1) * BC].rearrange("p b w -> p (b w)"),
                       start=True, stop=True).then_inc(s_d, 1)
                if k >= 1:
                    pe.wait_ge(s_sq, k)
                    mm(banks[4 + (k - 1) % 4][:, 0:NC], mean_w[:, :], early[:, 0, (k - 1) % 4],
                       start=True, stop=True).then_inc(s_v, 1)
            pe.wait_ge(s_xn, 2 + 2 * CH)

            for n in range(8):
                k = n // 2
                shifts = list(enumerate(SHIFTS))[0:4] if n % 2 == 0 else list(enumerate(SHIFTS))[4:SH]
                pe.wait_ge(s_tape, 2 * k + 2)
                for si, s in shifts:
                    t = 2 * s + TAPS // 2
                    taps = tape[:, k, t:t + 2].rearrange("p a c -> p (a c)")
                    last = nc.tensor.transpose(banks[n][:, (si % 4) * P:(si % 4 + 1) * P], taps, ident[:, :])
                last.then_inc(s_wt, 1)

            pe.wait_ge(s_eraw, 6 * 16)
            pe.wait_ge(s_wh, 8)
            pe.wait_ge(s_wv, 4)
            mm(banks[SUM[0]][:, 0:E * C], mean_w[:, :], ew[:, 0:E * C], start=True, stop=True)
            mm(banks[SUM[1]][:, 0:E], mean_w[:, :], ew[:, E * C:], start=True, stop=True).then_inc(s_cmean, 1)

            def row_step(t, k, g, middle=lambda: None):
                acc = banks[CONV[g]][:, 0:NV].rearrange("p (b w) -> p b w", b=BG)

                def taps(wpart, cpart, first, final):
                    for si, s in enumerate(SHIFTS):
                        lo, hi = (max(0, -s), min(WP, WP - s)) if abs(s) != 1 else (0, WP)
                        last = mm(acc[:, :, lo:hi], vw[:, k, wpart, si], carry[:, cpart, g, :, lo + s + 1:hi + s + 1],
                                  start=first and si == 0, stop=final and si == SH - 1)
                    return last

                pe.wait_ge(s_h[g], t)
                taps(0, 0, True, False)
                taps(1, 0, False, False)
                middle()
                pe.wait_ge(s_l[g], t)
                taps(0, 1, False, True).then_inc(s_mm[g], 1)

            def down_pair(i, before, norm):
                for m in range(CH):
                    n = CH * (i + 2) + m

                    def middle():
                        if m > 0 and norm or m == 0 and before:
                            variance(n - 1, (m - 1) % 2)
                    row_step(2 * i + 1 + m // G, 0, m % G, middle)
                    if norm:
                        center(n, m % 2)

            pe.wait_ge(s_cr, 2)
            down_pair(0, False, True)
            down_pair(1, True, True)
            with pe.Fori(2, HP - 2) as i:
                down_pair(i, True, True)
            down_pair(HP - 2, True, False)
            for g in range(G):
                row_step(H - 1, 0, g)
            with pe.Fori(H, 2 * H - 2) as t:
                for g in range(G):
                    row_step(t, 1, g)

            def col_step(u, k):
                for g in range(G):
                    pe.wait_ge(s_k[g], u)
                    for si, s in enumerate(SHIFTS):
                        lo, hi = max(0, -s), min(HP, HP - s)
                        last = mm(banks[CONV[g]][:, lo * BG:hi * BG], hw[:, k, si],
                                  kbuf[:, g, lo + s:hi + s].rearrange("p j b -> p (j b)"),
                                  start=si == 0, stop=si == SH - 1)
                    last.then_inc(s_hm[g], 1)

            with pe.Fori(1, W) as u:
                col_step(u, 0)
            with pe.Fori(W, 2 * W - 2) as u:
                col_step(u, 1)

            def center_tokens(j, c, bank=None):
                n = CH * j + c
                pe.wait_ge(s_t, n + 1)
                if bank is None and c > 0:
                    pe.wait_ge(s_ln2, n)
                elif bank is None and later(j):
                    pe.wait_ge(s_sm, SMN * (j - 1) + 1)
                dst = banks[TLN[c % 2] if bank is None else bank]
                mm(dst[:, 0:NC], center_w[:, :], cols[:, j, c * BC:(c + 1) * BC].rearrange("p b w -> p (b w)"),
                   start=True, stop=True).then_inc(s_d2, 1)

            def variance_tokens(j, c, bank=None):
                n = CH * j + c
                pe.wait_ge(s_sq2, n + 1)
                if bank is None:
                    pe.wait_ge(s_xn2, n)
                dst = banks[TLN[1 - c % 2] if bank is None else bank]
                mm(dst[:, 0:NC], mean_w[:, :], sq[:, c % 2], start=True, stop=True).then_inc(s_v2, 1)

            def tile_lo(p):
                return min(p * TN, REG - TN)

            def logits(j, slot, c):
                pe.wait_ge(s_tl, 2 * (CH * j + c + 1))
                if c == 0:
                    pe.wait_ge(s_ln2, CH * (j + 1))
                for p in range(TILES):
                    if c * NC < tile_lo(p) + TN <= (c + 1) * NC:
                        for q in range(2):
                            k = 2 * E * (2 * p + q)
                            last = mm(banks[LOG][:, k:k + 2 * E], tok[:, slot, q, tile_lo(p):tile_lo(p) + TN],
                                      rm[:, :, :].rearrange("p l e -> p (l e)"), start=True, stop=True)
                if c == CH - 1:
                    last.then_inc(s_lt, 1)

            def experts(j, slot, p):
                n, span = TILES * j + p, slice(tile_lo(p), tile_lo(p) + TN)
                for q in range(2):
                    sem_g, engine = (s_ga, "act") if q == 1 and (p - 2) % TILES in ACT_TILES else (s_g, "dve")
                    if p >= 2:
                        pe.wait_ge(sem_g, gates(engine, j, p - 2, q))
                    elif later(j):
                        pe.wait_ge(sem_g, gates(engine, j - 1, p - 2 + TILES, q))
                    for b in range(2):
                        last = mm(banks[OUTS[(TILES * slot + p) % 2][q]][:, 0:E * C], tok[:, slot, q, span], em[:, b],
                                  start=b == 0, stop=b == 1)
                    last.then_inc(s_p, 1)

            def sum_experts(j, slot, p):
                n = TILES * j + p
                pe.wait_ge(s_ps, n + 1)
                pe.wait_ge(s_o, n + 1)
                for e in range(E // 2):
                    last = mm(banks[SUM[(TILES * slot + p) % 2]][:, 0:TN], stage(slot, p)[:, e], ident[:, :],
                              start=e == 0, stop=e == E // 2 - 1, is_transpose=True)
                last.then_inc(s_y, 1)

            def region(j, slot, now, ahead):
                for p in range(TILES):
                    if j is not None:
                        experts(j, slot, p)
                    if now is not None:
                        if j is not None and p in (1, 3):
                            variance_tokens(now, (p + 3) // 2)
                        if j is not None and p in (0, 2):
                            center_tokens(now, p // 2 + 2)
                        for c in range(CH):
                            if p == LOGITS_AT[c]:
                                logits(now, 1 - slot, c)
                    if ahead is not None:
                        if p == 9:
                            center_tokens(ahead, 0)
                        if p in (10, 12):
                            variance_tokens(ahead, p // 2 - 5)
                        if p == 11:
                            center_tokens(ahead, 1)
                    if j is not None:
                        if p >= LAG:
                            sum_experts(j, slot, p - LAG)
                        elif later(j):
                            sum_experts(j - 1, 1 - slot, TILES + p - LAG)

            pe.wait_ge(s_em, 7)
            center_tokens(0, 0, 0)
            for c in range(CH):
                if c < CH - 1:
                    center_tokens(0, c + 1, c + 1)
                variance_tokens(0, c, TLN[0] + c)
            region(None, 1, 0, 1)
            region(0, 0, 1, 2)
            with pe.Fori(1, HP // 2 - 1) as i:
                region(2 * i - 1, 1, 2 * i, 2 * i + 1)
                region(2 * i, 0, 2 * i + 1, 2 * i + 2)
            region(HP - 3, 1, HP - 2, HP - 1)
            region(HP - 2, 0, HP - 1, None)
            region(HP - 1, 1, None, None)
            for p in range(TILES - LAG, TILES):
                sum_experts(HP - 1, 1, p)


_INS = ['x', 'L0_conv_w_d', 'L0_conv_w_u', 'L0_conv_w_r', 'L0_conv_w_l',
        'L0_ffn_router_w', 'L0_ffn_router_b', 'L0_ffn_expert_w', 'L0_ffn_expert_b']


def kernel(**inputs):
    import numpy as np
    import concourse.bacc as bacc
    from concourse.bass_utils import run_bass_kernel_spmd

    nc = bacc.Bacc("TRN2", target_bir_lowering=False, num_devices=1)
    arrays, args = {}, []
    for name in _INS:
        a = np.ascontiguousarray(inputs[name])
        arrays[name] = a
        args.append(nc.dram_tensor(name, a.shape, mybir.dt.from_np(a.dtype), kind="ExternalInput").ap())
    shape = arrays['x'].shape
    args.append(nc.dram_tensor("result", shape, F32, kind="ExternalOutput").ap())
    metaformer_kernel(nc, *args)
    r = run_bass_kernel_spmd(nc, [arrays], core_ids=[0])
    return r.results[0]["result"]
```
